# Optimizing a Trainium2 kernel written in Bass

```python
import numpy as np
import jax
import jax.numpy as jnp

def _softmax(x, axis=-1):
    return jax.nn.softmax(x, axis=axis)

def _gelu(x):
    return jax.nn.gelu(x, approximate=True)

def _silu(x):
    return jax.nn.silu(x)

def _sigmoid(x):
    return jax.nn.sigmoid(x)

def _layernorm(x, axis=-1, eps=1e-05):
    m = jnp.mean(x, axis=axis, keepdims=True)
    v = jnp.var(x, axis=axis, keepdims=True)
    return (x - m) / jnp.sqrt(v + eps)

def _scatter_add(tgt, idx, src, axis=0):
    return tgt.at[idx].add(src)

def _segment_sum(src, seg, n):
    return jax.ops.segment_sum(src, seg, n)
kernel_name = 'mk_xattn_ffn_d1_seqx_r4_b41011'

def setup_inputs(seed: int=0):
    np.random.seed(seed)
    _w = jnp.asarray

    def _rec_inputs():
        import jax
        import jax.numpy as jnp
        _rk = jax.random.key(seed)
        x = -0.0005207 + 1.001 * jax.random.normal(jax.random.fold_in(_rk, 1), (16, 100, 1024), jnp.float32)
        _lenS = 100 - jax.random.randint(jax.random.fold_in(_rk, 7), (16,), 0, max(1, 100 // 4) + 1, jnp.int32)
        _lenS2 = 361 - jax.random.randint(jax.random.fold_in(_rk, 8), (16,), 0, max(1, 361 // 4) + 1, jnp.int32)
        _ctx_4096P = jax.random.normal(jax.random.fold_in(_rk, 11), (16, 16, 1024), jnp.float32)
        _ctx_4096c = jax.random.dirichlet(jax.random.fold_in(_rk, 511), 0.3 * jnp.ones((16,), jnp.float32), (16, 361))
        _ctx_4096t = jnp.einsum('bsk,bkd->bsd', _ctx_4096c, _ctx_4096P)
        _ctx_4096t = _ctx_4096t * jax.lax.rsqrt(jnp.mean(jnp.square(_ctx_4096t)) + 1e-12) * 0.953939
        ctx_4096 = -0.00010331 + 0.999899 * (_ctx_4096t + 0.3 * jax.random.normal(jax.random.fold_in(_rk, 611), (16, 361, 1024), jnp.float32))
        return (x, ctx_4096)
    x, ctx_4096 = _rec_inputs()

    def _L0_xattn_setup():
        import jax, jax.numpy as jnp
        import numpy as np
        import math
        HIDDEN = 1024
        N_HEADS = 32
        HEAD_DIM = 128
        N_KV_HEADS = 4
        N_GROUPS = N_HEADS // N_KV_HEADS
        key = jax.random.key(seed)
        ks = jax.random.split(key, 6)
        B, NL, S = (8, 64, 1024)
        latents = jax.random.normal(ks[0], (B, NL, HIDDEN), dtype=jnp.float32)
        context = jax.random.normal(ks[1], (B, S, HIDDEN), dtype=jnp.float32)
        scale = 1.0 / math.sqrt(HIDDEN)
        Wq = jax.random.normal(ks[2], (HIDDEN, N_HEADS * HEAD_DIM), dtype=jnp.float32) * scale
        Wk = jax.random.normal(ks[3], (HIDDEN, N_KV_HEADS * HEAD_DIM), dtype=jnp.float32) * scale
        Wv = jax.random.normal(ks[4], (HIDDEN, N_KV_HEADS * HEAD_DIM), dtype=jnp.float32) * scale
        Wo = jax.random.normal(ks[5], (N_HEADS * HEAD_DIM, HIDDEN), dtype=jnp.float32) * scale
        return {'latents': latents, 'context': context, 'Wq': Wq, 'Wk': Wk, 'Wv': Wv, 'Wo': Wo}
    _L0_xattn_all = _L0_xattn_setup()
    _L0_xattn_in = {k: v for k, v in _L0_xattn_all.items() if k in ('Wq', 'Wk', 'Wv', 'Wo')}
    del _L0_xattn_all

    def _L0_ffn_setup():
        import jax, jax.numpy as jnp
        import numpy as np
        DIM = 1024
        INTER = 3584
        SPARSITY = 64
        RANK = 16
        key = jax.random.key(seed)
        ks = jax.random.split(key, 5)
        B, T = (64, 1)
        x = jax.random.normal(ks[0], (B, T, DIM), dtype=jnp.float32)
        c1_w = jax.random.normal(ks[1], (RANK, DIM), dtype=jnp.float32) * (1.0 / np.sqrt(DIM))
        c2_w = jax.random.normal(ks[2], (INTER, RANK), dtype=jnp.float32) * (1.0 / np.sqrt(RANK))
        w1 = jax.random.normal(ks[3], (INTER, DIM), dtype=jnp.float32) * (1.0 / np.sqrt(DIM))
        w2t = jax.random.normal(ks[4], (INTER, DIM), dtype=jnp.float32) * (1.0 / np.sqrt(INTER))
        return {'x': x, 'c1_w': c1_w, 'c2_w': c2_w, 'w1': w1, 'w2t': w2t}
    _L0_ffn_all = _L0_ffn_setup()
    _L0_ffn_in = {k: v for k, v in _L0_ffn_all.items() if k in ('c1_w', 'c2_w', 'w1', 'w2t')}
    del _L0_ffn_all
    return {'x': x, 'ctx_4096': ctx_4096, 'L0_xattn_Wq': _L0_xattn_in['Wq'], 'L0_xattn_Wk': _L0_xattn_in['Wk'], 'L0_xattn_Wv': _L0_xattn_in['Wv'], 'L0_xattn_Wo': _L0_xattn_in['Wo'], 'L0_ffn_c1_w': _L0_ffn_in['c1_w'], 'L0_ffn_c2_w': _L0_ffn_in['c2_w'], 'L0_ffn_w1': _L0_ffn_in['w1'], 'L0_ffn_w2t': _L0_ffn_in['w2t']}

def reference(x, ctx_4096, L0_xattn_Wq, L0_xattn_Wk, L0_xattn_Wv, L0_xattn_Wo, L0_ffn_c1_w, L0_ffn_c2_w, L0_ffn_w1, L0_ffn_w2t):
    import jax
    import jax.numpy as jnp

    def _L0_xattn_ref(latents, context, Wq, Wk, Wv, Wo):
        import jax, jax.numpy as jnp
        import numpy as np
        import math
        HIDDEN = 1024
        N_HEADS = 32
        HEAD_DIM = 128
        N_KV_HEADS = 4
        N_GROUPS = N_HEADS // N_KV_HEADS
        b, q_len, _ = latents.shape
        kv_len = q_len + context.shape[1]
        hidden_states = jnp.concatenate([context, latents], axis=1)
        q = (latents @ Wq).reshape(b, q_len, N_KV_HEADS, N_GROUPS, HEAD_DIM)
        k = (hidden_states @ Wk).reshape(b, kv_len, N_KV_HEADS, HEAD_DIM)
        v = (hidden_states @ Wv).reshape(b, kv_len, N_KV_HEADS, HEAD_DIM)
        scale = 1.0 / math.sqrt(HEAD_DIM)
        scores = jnp.einsum('bqhgd,bkhd->bhgqk', q, k) * scale
        attn = jax.nn.softmax(scores.astype(jnp.float32), axis=-1).astype(q.dtype)
        out = jnp.einsum('bhgqk,bkhd->bqhgd', attn, v)
        out = out.reshape(b, q_len, N_HEADS * HEAD_DIM)
        return out @ Wo

    def _L0_ffn_ref(x, c1_w, c2_w, w1, w2t):
        import jax, jax.numpy as jnp
        import numpy as np
        DIM = 1024
        INTER = 3584
        SPARSITY = 64
        RANK = 16
        B, T, M = x.shape
        xf = x.reshape(B * T, M)
        inter = xf @ c1_w.T @ c2_w.T
        n_blocks = INTER // SPARSITY
        blk = inter.reshape(B * T, n_blocks, SPARSITY)
        idx = jnp.argmax(blk, axis=-1) + jnp.arange(0, INTER, SPARSITY)
        w1_g = w1[idx]
        w2_g = w2t[idx]
        h = jax.nn.relu(jnp.einsum('bkm,bm->bk', w1_g, xf))
        out = jnp.einsum('bk,bkm->bm', h, w2_g)
        return out.reshape(B, T, M)
    x = x + _L0_xattn_ref(_layernorm(x, axis=-1), ctx_4096, L0_xattn_Wq, L0_xattn_Wk, L0_xattn_Wv, L0_xattn_Wo)
    x = x + _L0_ffn_ref(_layernorm(x, axis=-1), L0_ffn_c1_w, L0_ffn_c2_w, L0_ffn_w1, L0_ffn_w2t)
    return x

_drawn_inputs = setup_inputs


def setup_inputs(seed=0):
    import zlib

    import numpy as np

    out = dict(_drawn_inputs(seed))
    spreads = {}
    factors = {}
    for name, (base, spread) in spreads.items():
        noise = np.random.default_rng([zlib.crc32(name.encode()), seed]).standard_normal(out[name].shape)
        drawn = base * np.exp(spread * noise) if base else spread * noise
        out[name] = jnp.asarray(drawn.astype(out[name].dtype))
    for name, factor in factors.items():
        out[name] = (out[name] * factor).astype(out[name].dtype)
    return out
```

```python
from contextlib import ExitStack

import concourse.bass as bass
from concourse import mybir

ALU = mybir.AluOpType
ACT = mybir.ActivationFunctionType
AX = mybir.AxisListType
F32 = mybir.dt.float32
F32R = mybir.dt.float32r
BF16 = mybir.dt.bfloat16

P = 128
EPS = 1e-5
PAIRS = ((0, 0), (0, 1), (1, 0))




def product(pe, out, left, right, chunks):
    for c in range(chunks):
        for a, b in PAIRS:
            last = pe.matmul(out, left(a, c), right(b, c),
                             start=(c == 0 and (a, b) == PAIRS[0]),
                             stop=(c == chunks - 1 and (a, b) == PAIRS[-1]))
    return last


def make_identity(nc, ident, ident_bf, made):
    with nc.Block() as block:
        @block.gpsimd
        def _(pool):
            pool.memset(ident[:, :], 0.0).then_inc(made, 1)
            pool.wait_ge(made, 1)
            pool.affine_select(out=ident[:, :], in_=ident[:, :], compare_op=ALU.not_equal, fill=1.0,
                               base=0, pattern=[[-1, P]], channel_multiplier=1).then_inc(made, 1)
            pool.wait_ge(made, 2)
            pool.tensor_copy(ident_bf[:, :], ident[:, :]).then_inc(made, 1)


def split_kv_weights(nc, sem, sources, wkv):
    landed = [sem("key_weights_landed"), sem("value_weights_landed")]
    high, low = sem("kvw_high"), sem("kvw_low")
    chunks, width = wkv.shape[3], wkv.shape[4]
    with ExitStack() as mem:
        raw = mem.enter_context(nc.sbuf_tensor("kvw_raw", [P, 2, chunks, width], F32))
        block = mem.enter_context(nc.Block())

        @block.sync
        def _(sp):
            for w, source in enumerate(sources):
                sp.dma_start(raw[:, w], source.rearrange("(c p) n -> p c n", p=P)).then_inc(landed[w], 16)

        @block.scalar
        def _(act):
            for w in range(2):
                act.wait_ge(landed[w], 16)
                act.activation(wkv[:, w, 0], raw[:, w], ACT.Copy).then_inc(high, 1)

        @block.vector
        def _(dve):
            for w in range(2):
                dve.wait_ge(high, w + 1)
                dve.tensor_tensor(wkv[:, w, 1], raw[:, w], wkv[:, w, 0].bitcast(F32),
                                  ALU.subtract).then_inc(low, 1)


def normalise(nc, sem, name, source, xt, ident):
    batches, rows, hidden = source.shape
    chunks = hidden // P
    half = hidden // 2
    landed, used = [sem(f"{name}_landed{i}") for i in range(2)], sem(name + "_used")
    step, rooted = sem(name + "_step"), sem(name + "_rooted")
    ready, turned = sem(name + "_ready"), sem(name + "_turned")
    high, low = sem(name + "_high"), sem(name + "_low")
    waited = sem(name + "_waited")
    STEPS = 7

    with ExitStack() as mem:
        def sb(n, shape, dt=F32):
            return mem.enter_context(nc.sbuf_tensor(f"{name}_{n}", shape, dt))

        raw = [sb(f"raw{i}", [P, hidden]) for i in range(2)]
        xn = [sb(f"xn{i}", [P, hidden]) for i in range(2)]
        stats = [sb(f"stats{i}", [P, 2, 6]) for i in range(2)]
        moments = [sb(f"moments{i}", [P, 2]) for i in range(2)]
        small = [sb(f"small{i}", [P, 6]) for i in range(2)]
        turned_ps = [mem.enter_context(nc.psum_tensor(f"{name}_ps{i}", [P, chunks, P], F32)) for i in range(2)]
        block = mem.enter_context(nc.Block())

        @block.sync
        def _(sp):
            for b in range(2):
                sp.dma_start(raw[b][:rows, :], source[b]).then_inc(landed[b], 16)
            with sp.Fori(0, batches // 2 - 1) as i:
                for b in range(2):
                    sp.wait_ge(used, 2 * i + b + 1)
                    sp.dma_start(raw[b][:rows, :],
                                 source[bass.ds(2 * i + b + 2, 1)].rearrange("a r n -> (a r) n")).then_inc(landed[b], 16)

        @block.vector
        def _(dve):
            def norm(k, p):
                b = 2 * k + p
                v, m, s = small[p], moments[p], stats[p]
                dve.wait_ge(landed[p], 16 * (k + 1))
                for c in range(2):
                    last = dve.bn_stats(s[:rows, c, :], raw[p][:rows, c * half:(c + 1) * half])
                last.then_inc(step, 1)
                dve.wait_ge(step, STEPS * b + 1)
                dve.sem_inc(waited, 1)
                dve.bn_aggr(m[:rows, :], s[:rows, :, :]).then_inc(step, 1)
                dve.wait_ge(step, STEPS * b + 2)
                dve.tensor_scalar(v[:rows, 0:1], m[:rows, 1:2], EPS, None, ALU.add).then_inc(step, 1)
                dve.wait_ge(rooted, b + 1)
                dve.reciprocal(v[:rows, 2:3], v[:rows, 1:2]).then_inc(step, 1)
                dve.wait_ge(step, STEPS * b + 4)
                dve.scalar_tensor_tensor(out=v[:rows, 3:4], in0=v[:rows, 2:3], scalar=v[:rows, 2:3],
                                         in1=v[:rows, 0:1], op0=ALU.mult, op1=ALU.mult).then_inc(step, 1)
                dve.wait_ge(step, STEPS * b + 5)
                dve.tensor_scalar(v[:rows, 4:5], v[:rows, 3:4], -0.5, 1.5, ALU.mult, ALU.add).then_inc(step, 1)
                dve.wait_ge(step, STEPS * b + 6)
                dve.tensor_tensor(v[:rows, 5:6], v[:rows, 2:3], v[:rows, 4:5], ALU.mult).then_inc(step, 1)
                dve.wait_ge(step, STEPS * b + 7)
                dve.tensor_scalar(xn[p][:rows, :], raw[p][:rows, :], m[:rows, 0:1], v[:rows, 5:6],
                                  ALU.subtract, ALU.mult).then_inc(ready, 1)

            def low_part(b, p):
                dve.wait_ge(high, b + 1)
                at = slice(b * rows, b * rows + rows) if isinstance(b, int) else bass.ds(b * rows, rows)
                dve.tensor_tensor(xt[:, 1, :, at], turned_ps[p][:, :, :rows], xt[:, 0, :, at].bitcast(F32),
                                  ALU.subtract).then_inc(low, 1)

            norm(0, 0)
            with dve.Fori(0, batches // 2 - 1) as i:
                norm(i, 1)
                low_part(2 * i, 0)
                norm(i + 1, 0)
                low_part(2 * i + 1, 1)
            norm(batches // 2 - 1, 1)
            low_part(batches - 2, 0)
            low_part(batches - 1, 1)

        @block.gpsimd
        def _(pool):
            with pool.Fori(0, batches) as i:
                pool.wait_ge(ready, i + 1)
                pool.sem_inc(used, 1)

        @block.scalar
        def _(act):
            def root(b, p):
                act.wait_ge(step, STEPS * b + 3)
                act.activation(small[p][:rows, 1:2], small[p][:rows, 0:1], ACT.Sqrt).then_inc(rooted, 1)

            def high_part(b, p):
                act.wait_ge(turned, b + 1)
                at = slice(b * rows, b * rows + rows) if isinstance(b, int) else bass.ds(b * rows, rows)
                act.activation(xt[:, 0, :, at], turned_ps[p][:, :, :rows], ACT.Copy).then_inc(high, 1)

            root(0, 0)
            with act.Fori(0, batches // 2 - 1) as i:
                root(2 * i + 1, 1)
                high_part(2 * i, 0)
                root(2 * i + 2, 0)
                high_part(2 * i + 1, 1)
            root(batches - 1, 1)
            high_part(batches - 2, 0)
            high_part(batches - 1, 1)

        @block.tensor
        def _(pe):
            def turn(b, p):
                pe.wait_ge(ready, b + 1)
                for c in range(chunks):
                    last = pe.transpose(turned_ps[p][:, c, :rows], xn[p][:rows, c * P:(c + 1) * P],
                                        ident[:rows, :rows])
                last.then_inc(turned, 1)

            turn(0, 0)
            turn(1, 1)
            with pe.Fori(0, batches // 2 - 1) as i:
                for p in range(2):
                    pe.wait_ge(low, 2 * i + p + 1)
                    turn(2 * i + p + 2, p)


def project_queries(nc, sem, wq, xt, q_dram, xt_dram, scale, batches, rows):
    hidden = wq.shape[0]
    chunks = hidden // P
    heads = q_dram.shape[2]
    tokens = batches * rows
    tiles, width = 4, tokens // 4
    landed = [sem(f"wq_landed{i}") for i in range(2)]
    high, low = sem("wq_high"), sem("wq_low")
    summed = sem("q_summed")
    out_act, out_dve = sem("q_out_act"), sem("q_out_dve")
    stage_free, saved = [sem(f"q_stage_free{i}") for i in range(2)], sem("xt_saved")

    with ExitStack() as mem:
        def sb(n, shape, dt=F32):
            return mem.enter_context(nc.sbuf_tensor(n, shape, dt))

        raw = [sb(f"wq_raw{i}", [P, chunks, P]) for i in range(2)]
        w = [sb(f"wq_parts{i}", [P, 2, chunks, P], F32R) for i in range(2)]
        stage = [sb(f"q_stage{i}", [P, tokens]) for i in range(2)]
        acc = mem.enter_context(nc.psum_tensor("q_acc", [P, 2, tiles, 512], F32))
        block = mem.enter_context(nc.Block())
        wq_v = wq.rearrange("(c p) n -> p c n", p=P)
        q_v = q_dram.rearrange("b d h r -> h d b r")

        @block.sync
        def _(sp):
            def load(h, p):
                at = slice(h * P, (h + 1) * P) if isinstance(h, int) else bass.ds(h * P, P)
                sp.dma_start(raw[p][:, :, :], wq_v[:, :, at]).then_inc(landed[p], 16)

            def store(h, p):
                sp.wait_ge(out_act, 2 * h + 2 + 4)
                sp.wait_ge(out_dve, 2 * h + 2 + 4)
                sp.dma_start(q_v[bass.ds(h, 1)].rearrange("a d b r -> (a d) b r"),
                             stage[p][:, :].rearrange("p (b r) -> p b r", b=batches)).then_inc(stage_free[p], 16)

            load(0, 0)
            load(1, 1)
            for part in range(2):
                sp.dma_start(xt_dram[part], xt[:, part].bitcast(F32)).then_inc(saved, 16)
            with sp.Fori(0, heads // 2 - 1) as i:
                for p in range(2):
                    sp.wait_ge(low, 2 * i + p + 1)
                    load(2 * i + p + 2, p)
                    store(2 * i + p, p)
            store(heads - 2, 0)
            store(heads - 1, 1)
            for p in range(2):
                sp.wait_ge(stage_free[p], 16 * (heads // 2 + 1))
            sp.wait_ge(saved, 32)

        @block.gpsimd
        def _(pool):
            pool.sem_inc(stage_free[0], 16)
            pool.sem_inc(stage_free[1], 16)
            pool.sem_inc(out_act, 4)
            pool.sem_inc(out_dve, 4)

        @block.scalar
        def _(act):
            def split(k, p):
                act.wait_ge(landed[p], 16 * (k + 1))
                act.activation(w[p][:, 0], raw[p][:, :, :], ACT.Copy).then_inc(high, 1)

            def evacuate(k, p):
                h = 2 * k + p
                act.wait_ge(stage_free[p], 16 * (k + 1))
                for t in (0, 2):
                    act.wait_ge(summed, tiles * h + t + 1)
                    act.activation(stage[p][:, t * width:(t + 1) * width], acc[:, p, t, :width], ACT.Copy,
                                   scale=scale).then_inc(out_act, 1)

            split(0, 0)
            split(0, 1)
            with act.Fori(0, heads // 2 - 1) as i:
                for p in range(2):
                    evacuate(i, p)
                    act.wait_ge(summed, tiles * (2 * i + p + 1))
                    split(i + 1, p)
            evacuate(heads // 2 - 1, 0)
            evacuate(heads // 2 - 1, 1)

        @block.vector
        def _(dve):
            def split(k, p):
                dve.wait_ge(high, 2 * k + p + 1)
                dve.tensor_tensor(w[p][:, 1], raw[p][:, :, :], w[p][:, 0].bitcast(F32),
                                  ALU.subtract).then_inc(low, 1)

            def evacuate(k, p):
                h = 2 * k + p
                dve.wait_ge(stage_free[p], 16 * (k + 1))
                for t in (1, 3):
                    dve.wait_ge(summed, tiles * h + t + 1)
                    dve.tensor_scalar(stage[p][:, t * width:(t + 1) * width], acc[:, p, t, :width], scale, None,
                                      ALU.mult).then_inc(out_dve, 1)

            split(0, 0)
            split(0, 1)
            with dve.Fori(0, heads // 2 - 1) as i:
                for p in range(2):
                    evacuate(i, p)
                    split(i + 1, p)
            evacuate(heads // 2 - 1, 0)
            evacuate(heads // 2 - 1, 1)

        @block.tensor
        def _(pe):
            with pe.Fori(0, heads // 2) as i:
                for p in range(2):
                    h = 2 * i + p
                    pe.wait_ge(low, h + 1)
                    for t in range(tiles):
                        pe.wait_ge(out_act if t % 2 == 0 else out_dve, 2 * h + t // 2 + 1)
                        product(pe, acc[:, p, t, :width], lambda a, c: w[p][:, a, c, :],
                                lambda a, c: xt[:, a, c, t * width:(t + 1) * width], chunks).then_inc(summed, 1)


def attend(nc, sem, ctx, xt_dram, q_dram, wkv, o_dram, ident):
    batches, keys_ctx, hidden = ctx.shape
    _, d, heads, rows = q_dram.shape
    groups = wkv.shape[4] // d
    per = heads // groups
    chunks = hidden // P
    kv = keys_ctx + rows
    kvp = kv + kv % 2
    row_chunks = [(c * P, min(P, keys_ctx - c * P)) for c in range((keys_ctx + P - 1) // P)]
    kv_chunks = [(c * P, min(P, kv - c * P)) for c in range((kv + P - 1) // P)]
    NC = len(kv_chunks)
    full = keys_ctx // P
    cols = per * rows
    half = cols // 2
    tile = 116
    tiles = [(t * tile, min(tile, cols - t * tile)) for t in range((cols + tile - 1) // tile)]
    NT = len(tiles)
    N = groups * NT
    first_o = chunks + groups + NC
    U = first_o + 2 * groups
    SB, TB, JB, RB, LAG = 3, 2, 3, 4, 3
    half_at = [max(t for t, (a, _) in enumerate(tiles) if a < half) + 1, NT]
    assert U % JB == 0 and tile * 4 <= 512 and NC == 4

    ctx_landed, lat_landed, q_landed = sem("ctx_landed"), sem("lat_landed"), [sem(f"q_landed{i}") for i in range(2)]
    shared_full, shared_high, shared_free = sem("shared_full"), sem("shared_high"), sem("shared_free")
    q_high, q_split = sem("q_high"), sem("q_split")
    s_full, s_max, exped = sem("s_full"), sem("s_max"), sem("exped")
    inverted, scaled = sem("inverted"), sem("scaled")
    pt_full, pt_high, pt_low = sem("pt_full"), sem("pt_high"), sem("pt_low")
    o_free = [sem(f"o_free{i}") for i in range(2)]
    cleared, waited = sem("attend_cleared"), sem("attend_waited")

    with ExitStack() as mem:
        def sb(n, shape, dt=F32):
            return mem.enter_context(nc.sbuf_tensor(n, shape, dt))

        ctx_raw = sb("ctx_raw", [P, len(row_chunks), hidden])
        hst = sb("hst", [P, 2, chunks, kvp], F32R)
        kt = sb("kt", [P, 2, groups, kvp], F32R)
        v = sb("v", [P, 2, NC, groups * P], F32R)
        q_raw = [sb(f"q_raw{i}", [P, cols]) for i in range(2)]
        q = [sb(f"q_parts{i}", [P, 2, cols], F32R) for i in range(2)]
        probs = sb("probs", [P, RB, NC * P])
        pt = sb("pt", [P, 2, NC, cols], F32R)
        o = [sb(f"o_stage{i}", [P, cols]) for i in range(2)]
        negmax = sb("negmax", [P, RB])
        total = sb("total", [P, RB])
        inverse = sb("inverse", [P, RB])
        scores = mem.enter_context(nc.psum_tensor("scores", [P, SB, 512], F32))
        turned = mem.enter_context(nc.psum_tensor("turned", [P, TB, 512], F32))
        shared = mem.enter_context(nc.psum_tensor("shared", [P, JB, 512], F32))
        block = mem.enter_context(nc.Block())
        q_v = q_dram.rearrange("b d (g h) r -> g b d (h r)", g=groups)
        o_v = o_dram.rearrange("(g h) d (b r) -> g b d h r", g=groups, b=batches)

        def shared_bank(u):
            if u < chunks:
                return shared[:, u % JB, :keys_ctx]
            if u < chunks + groups:
                return shared[:, u % JB, :kvp]
            n = kv_chunks[u - chunks - groups][1]
            return shared[:n, u % JB, :]

        def shared_part(u, part, dt):
            if u < chunks:
                return hst[:, part, u, :keys_ctx].bitcast(dt)
            if u < chunks + groups:
                return kt[:, part, u - chunks, :].bitcast(dt)
            k = u - chunks - groups
            return v[:kv_chunks[k][1], part, k, :].bitcast(dt)

        def turned_tile(i, n):
            return turned[:, i % TB, :NC * tile].rearrange("p (k n) -> p k n", k=NC)[:, :, :n]

        @block.sync
        def _(sp):
            def load_ctx(b):
                rows_b = ctx[bass.ds(b, 1)].rearrange("a r n -> (a r) n")
                sp.dma_start(ctx_raw[:, :full, :],
                             rows_b[:full * P, :].rearrange("(c p) n -> p c n", p=P)).then_inc(ctx_landed, 16)
                sp.dma_start(ctx_raw[:keys_ctx - full * P, full, :], rows_b[full * P:, :]).then_inc(ctx_landed, 16)

            def load_q(b, g):
                sp.dma_start(q_raw[g % 2][:, :],
                             q_v[g, bass.ds(b, 1)].rearrange("a d n -> (a d) n")).then_inc(q_landed[g % 2], 16)

            def batch(b, last):
                sp.wait_ge(shared_free, U * b + JB)
                for part in range(2):
                    sp.dma_start(hst[:, part, :, keys_ctx:kv].bitcast(F32),
                                 xt_dram[part, :, :, bass.ds(b * rows, rows)]).then_inc(lat_landed, 16)
                load_q(b, 0)
                load_q(b, 1)
                if not last:
                    sp.wait_ge(shared_full, U * b + chunks)
                    load_ctx(b + 1)
                for g in range(2, groups):
                    sp.wait_ge(q_split, 2 * (groups * b + g - 1))
                    load_q(b, g)
                for g in range(groups):
                    sp.wait_ge(shared_free, U * b + first_o + 2 * g + 2 + JB)
                    sp.dma_start(o_v[g, bass.ds(b, 1)].rearrange("a d h r -> (a d) h r"),
                                 o[g % 2][:, :].rearrange("p (h r) -> p h r", h=per)).then_inc(o_free[g % 2], 16)

            load_ctx(0)
            with sp.Fori(0, batches - 1) as b:
                batch(b, False)
            batch(batches - 1, True)
            for p in range(2):
                sp.wait_ge(o_free[p], 16 * (1 + groups // 2 * batches))

        @block.gpsimd
        def _(pool):
            pool.memset(hst[:, :, :, kv:].bitcast(F32), 0.0).then_inc(cleared, 1)
            pool.memset(probs[:, :, :], 0.0).then_inc(cleared, 1)
            pool.sem_inc(shared_free, JB)
            pool.sem_inc(o_free[0], 16)
            pool.sem_inc(o_free[1], 16)

            def split_q(b, g, part, h):
                at = slice(h * half, (h + 1) * half)
                if part == 0 and h == 0:
                    pool.wait_ge(q_landed[g % 2], 16 * (groups // 2 * b + g // 2 + 1))
                    if g >= 2:
                        pool.wait_ge(s_full, N * b + NT * (g - 1))
                    pool.sem_inc(waited, 1)
                if part == 0:
                    pool.tensor_scalar(q[g % 2][:, 0, at], q_raw[g % 2][:, at], 1.0, 1.0,
                                       ALU.mult, ALU.mult).then_inc(q_high, 1)
                else:
                    pool.wait_ge(q_high, 2 * (groups * b + g) + h + 1)
                    pool.tensor_tensor(q[g % 2][:, 1, at], q_raw[g % 2][:, at], q[g % 2][:, 0, at].bitcast(F32),
                                       ALU.subtract).then_inc(q_split, 1)

            with pool.Fori(0, batches) as b:
                for g in range(2):
                    for h in range(2):
                        for part in range(2):
                            split_q(b, g, part, h)
                for i in range(N):
                    g, t = divmod(i, NT)
                    n = tiles[t][1]
                    pool.wait_ge(inverted, N * b + i + 1)
                    pool.sem_inc(waited, 1)
                    pool.tensor_scalar(probs[:n, i % RB, :kv], probs[:n, i % RB, :kv], inverse[:n, i % RB:i % RB + 1],
                                       1.0, ALU.mult, ALU.mult).then_inc(scaled, 1)
                    if 1 <= g and g + 1 < groups and 0 <= t - 1 < 4:
                        split_q(b, g + 1, (t - 1) % 2, (t - 1) // 2)

        @block.tensor
        def _(pe):
            pe.wait_ge(cleared, 2)
            with pe.Fori(0, batches) as b:
                def take(u):
                    pe.wait_ge(shared_free, U * b + u + 1)
                    return shared[:, u % JB]

                pe.wait_ge(ctx_landed, 32 * (b + 1))
                for c in range(chunks):
                    bank = take(c)
                    for r, (a, n) in enumerate(row_chunks):
                        last = pe.transpose(bank[:, a:a + n], ctx_raw[:n, r, c * P:(c + 1) * P], ident[:n, :n])
                    last.then_inc(shared_full, 1)
                pe.wait_ge(lat_landed, 32 * (b + 1))
                pe.wait_ge(shared_free, U * b + chunks + JB)
                for g in range(groups):
                    bank = take(chunks + g)
                    product(pe, bank[:, :kvp], lambda a, c: wkv[:, 0, a, c, g * P:(g + 1) * P],
                            lambda a, c: hst[:, a, c, :], chunks).then_inc(shared_full, 1)
                for k, (at, n) in enumerate(kv_chunks):
                    bank = take(chunks + groups + k)
                    product(pe, bank[:n, :], lambda a, c: hst[:, a, c, at:at + n],
                            lambda a, c: wkv[:, 1, a, c, :], chunks).then_inc(shared_full, 1)

                def score(i):
                    g, t = divmod(i, NT)
                    at, n = tiles[t]
                    if t == 0:
                        pe.wait_ge(q_split, 2 * (groups * b + g + 1))
                    if i >= SB:
                        pe.wait_ge(exped, N * b + i - SB + 1)
                    product(pe, scores[:n, i % SB, :kvp], lambda a, c: q[g % 2][:, a, at:at + n],
                            lambda a, c: kt[:, a, g, :], 1).then_inc(s_full, 1)

                def turn(i):
                    t = i % NT
                    n = tiles[t][1]
                    pe.wait_ge(scaled, N * b + i + 1)
                    if i >= TB:
                        pe.wait_ge(pt_low, N * b + i - TB + 1)
                    for k in range(NC):
                        last = pe.transpose(turned[:, i % TB, k * tile:k * tile + n],
                                            probs[:n, i % RB, k * P:(k + 1) * P], ident[:n, :n])
                    last.then_inc(pt_full, 1)

                def weigh(g, h):
                    pe.wait_ge(pt_low, N * b + NT * g + half_at[h])
                    bank = take(first_o + 2 * g + h)
                    for k, (at, n) in enumerate(kv_chunks):
                        for a, c in PAIRS:
                            last = pe.matmul(bank[:, :half], v[:n, a, k, g * P:(g + 1) * P],
                                             pt[:n, c, k, h * half:(h + 1) * half],
                                             start=(k == 0 and (a, c) == PAIRS[0]),
                                             stop=(k == NC - 1 and (a, c) == PAIRS[-1]))
                    last.then_inc(shared_full, 1)

                pe.wait_ge(shared_free, U * b + first_o + JB)
                for i in range(N + LAG + 2):
                    if i < N:
                        score(i)
                    j = i - LAG
                    if 0 <= j < N:
                        turn(j)
                    for g in range(groups):
                        for h in range(2):
                            if j == NT * g + half_at[h] + 1:
                                weigh(g, h)

        @block.scalar
        def _(act):
            with act.Fori(0, batches) as b:
                for u in range(first_o):
                    act.wait_ge(shared_full, U * b + u + 1)
                    act.activation(shared_part(u, 0, F32R), shared_bank(u), ACT.Copy).then_inc(shared_high, 1)
                for i in range(N + LAG):
                    j = i - LAG
                    if j >= 0:
                        at, n = tiles[j % NT]
                        act.wait_ge(pt_full, N * b + j + 1)
                        act.activation(pt[:, 0, :, at:at + n], turned_tile(j, n), ACT.Copy).then_inc(pt_high, 1)
                    if i < N:
                        n = tiles[i % NT][1]
                        act.wait_ge(s_max, N * b + i + 1)
                        if i >= RB:
                            act.wait_ge(pt_full, N * b + i - RB + 1)
                        act.activation(probs[:n, i % RB, :kv], scores[:n, i % SB, :kv], ACT.Exp,
                                       bias=negmax[:n, i % RB:i % RB + 1],
                                       accum_out=total[:n, i % RB:i % RB + 1]).then_inc(exped, 1)

        @block.vector
        def _(dve):
            with dve.Fori(0, batches) as b:
                for u in range(first_o):
                    dve.wait_ge(shared_high, first_o * b + u + 1)
                    dve.tensor_tensor(shared_part(u, 1, F32R), shared_bank(u), shared_part(u, 0, F32),
                                      ALU.subtract).then_inc(shared_free, 1)
                for i in range(N + LAG + 4):
                    if i < N:
                        n = tiles[i % NT][1]
                        dve.wait_ge(s_full, N * b + i + 1)
                        if i >= RB:
                            dve.wait_ge(exped, N * b + i - RB + 1)
                        dve.tensor_reduce(negmax[:n, i % RB:i % RB + 1], scores[:n, i % SB, :kv], AX.X, ALU.max,
                                          negate=True).then_inc(s_max, 1)
                    if 1 <= i < N + 1:
                        j = i - 1
                        n = tiles[j % NT][1]
                        dve.wait_ge(exped, N * b + j + 1)
                        if j >= RB:
                            dve.wait_ge(scaled, N * b + j - RB + 1)
                        dve.reciprocal(inverse[:n, j % RB:j % RB + 1],
                                       total[:n, j % RB:j % RB + 1]).then_inc(inverted, 1)
                    j = i - LAG
                    if 0 <= j < N:
                        at, n = tiles[j % NT]
                        dve.wait_ge(pt_high, N * b + j + 1)
                        dve.tensor_tensor(pt[:, 1, :, at:at + n], turned_tile(j, n),
                                          pt[:, 0, :, at:at + n].bitcast(F32), ALU.subtract).then_inc(pt_low, 1)
                    for g in range(groups):
                        for h in range(2):
                            if j == NT * g + half_at[h] + 2:
                                dve.wait_ge(shared_full, U * b + first_o + 2 * g + h + 1)
                                dve.wait_ge(o_free[g % 2], 16 * (groups // 2 * b + g // 2 + 1))
                                dve.tensor_copy(o[g % 2][:, h * half:(h + 1) * half],
                                                shared[:, (first_o + 2 * g + h) % JB, :half]).then_inc(shared_free, 1)



def gate_weights(nc, sem, c1, c2, x1t, c1t, c2t, z, ident):
    rank, hidden = c1.shape
    inter = c2.shape[0]
    chunks, blocks = hidden // P, inter // P
    tokens = x1t.shape[3]
    width = tokens // 4
    per = 4
    rounds = blocks // per
    cleared, landed = sem("gate_cleared"), sem("gate_landed")
    full, high, done = sem("gate_full"), sem("gate_high"), sem("gate_done")
    with ExitStack() as mem:
        c1_raw = mem.enter_context(nc.sbuf_tensor("c1_raw", [P, hidden], F32))
        c2_raw = mem.enter_context(nc.sbuf_tensor("c2_raw", [P, blocks, P], F32))
        banks = mem.enter_context(nc.psum_tensor("gate_banks", [P, 8, 512], F32))
        block = mem.enter_context(nc.Block())

        @block.gpsimd
        def _(pool):
            pool.memset(c1_raw[:, :], 0.0).then_inc(cleared, 1)
            pool.memset(c2_raw[:, :, :], 0.0).then_inc(cleared, 1)
            pool.memset(z[:, :], 0.0).then_inc(cleared, 1)

        @block.sync
        def _(sp):
            sp.wait_ge(cleared, 2)
            sp.dma_start(c1_raw[:rank, :], c1).then_inc(landed, 16)
            sp.dma_start(c2_raw[:, :, :rank], c2.rearrange("(j p) r -> p j r", p=P)).then_inc(landed, 16)

        @block.tensor
        def _(pe):
            pe.wait_ge(landed, 32)
            for h in range(2):
                for c in range(4):
                    last = pe.transpose(banks[:, h, c * P:(c + 1) * P],
                                        c1_raw[:, (4 * h + c) * P:(4 * h + c + 1) * P], ident[:, :])
                last.then_inc(full, 1)
            for r in range(rounds):
                if 2 + r >= 8:
                    pe.wait_ge(done, r - 5)
                for k in range(per):
                    last = pe.transpose(banks[:, (2 + r) % 8, k * P:(k + 1) * P], c2_raw[:, per * r + k, :], ident[:, :])
                last.then_inc(full, 1)
            for t in range(4):
                pe.wait_ge(done, 2 + t)
                product(pe, banks[:, 1 + t, :width], lambda a, c: c1t[:, a, c, :],
                        lambda a, c: x1t[:, a, c, t * width:(t + 1) * width], chunks).then_inc(full, 1)

        @block.scalar
        def _(act):
            for h in range(2):
                act.wait_ge(full, h + 1)
                act.activation(c1t[:, 0, 4 * h:4 * h + 4, :], banks[:, h, :].rearrange("p (c n) -> p c n", c=4),
                               ACT.Copy).then_inc(high, 1)

        @block.vector
        def _(dve):
            for h in range(2):
                dve.wait_ge(high, h + 1)
                dve.tensor_tensor(c1t[:, 1, 4 * h:4 * h + 4, :], banks[:, h, :].rearrange("p (c n) -> p c n", c=4),
                                  c1t[:, 0, 4 * h:4 * h + 4, :].bitcast(F32), ALU.subtract).then_inc(done, 1)
            for r in range(rounds):
                dve.wait_ge(full, 3 + r)
                dve.tensor_copy(c2t[:, r * 512:(r + 1) * 512], banks[:rank, (2 + r) % 8, :]).then_inc(done, 1)
            dve.wait_ge(cleared, 3)
            for t in range(4):
                dve.wait_ge(full, 3 + rounds + t)
                dve.tensor_copy(z[:, t * width:(t + 1) * width], banks[:rank, 1 + t, :width]).then_inc(done, 1)


def hidden_layer(nc, sem, w1, x1t, c2t, z, h_dram, ident, ident_bf, sparsity):
    inter, hidden = w1.shape
    chunks, blocks = hidden // P, inter // P
    tokens = x1t.shape[3]
    tiles = 4
    width = tokens // tiles
    tt = z.shape[1] // P
    tail = tokens - (tt - 1) * P
    first, second = 8, tt - 8
    per = P // sparsity
    landed, turned = [sem(f"w1_landed{i}") for i in range(2)], sem("w1_turned")
    high, low = sem("w1_high"), sem("w1_low")
    gated, compared, masked, step = sem("gated"), sem("compared"), sem("masked"), sem("mask_step")
    mask_turned, mask_out = sem("mask_turned"), sem("mask_out")
    summed, h_out, made = sem("h_summed"), sem("h_out"), sem("keys_made")
    stored = [sem(f"h_stored{i}") for i in range(2)]
    waited = sem("gate_waited")
    STEPS = 8

    with ExitStack() as mem:
        def sb(n, shape, dt=F32):
            return mem.enter_context(nc.sbuf_tensor("hid_" + n, shape, dt))

        raw = [sb(f"raw{i}", [P, hidden]) for i in range(2)]
        w = [sb(f"w{i}", [P, 2, chunks, P], F32R) for i in range(2)]
        top = sb("top", [P, tt * per])
        lead = sb("lead", [P, tt * per])
        keys = sb("keys", [P, sparsity])
        key_bf = sb("key_bf", [P, sparsity], BF16)
        equal = sb("equal", [P, tt * per, sparsity], BF16)
        mask = [sb(f"mask{i}", [P, tt * per, sparsity], BF16) for i in range(2)]
        mask_t = sb("mask_t", [P, tokens], BF16)
        h = [sb(f"h{i}", [P, tokens]) for i in range(2)]
        gate = mem.enter_context(nc.psum_tensor("gate", [P, 2, 512], F32))
        turn = mem.enter_context(nc.psum_tensor("turn", [P, 2, 512], F32))
        acc = mem.enter_context(nc.psum_tensor("hid_acc", [P, tiles, 512], F32))
        block = mem.enter_context(nc.Block())
        w1_v = w1.rearrange("(j p) n -> j p n", p=P)
        parts = ((0, first), (first, second))

        def over_blocks(eng, body):
            with eng.Fori(0, blocks // 2 - 1) as i:
                body(i, 0, True)
                body(i, 1, True)
            body(blocks // 2 - 1, 0, True)
            body(blocks // 2 - 1, 1, False)

        @block.sync
        def _(sp):
            def load(j, p):
                sp.dma_start(raw[p][:, :], w1_v[bass.ds(j, 1)].rearrange("a p n -> (a p) n")).then_inc(landed[p], 16)

            def store(j, p):
                sp.wait_ge(h_out, tiles * (j + 2))
                sp.dma_start(h_dram[bass.ds(j, 1)].rearrange("a p n -> (a p) n"), h[p][:, :]).then_inc(stored[p], 16)

            load(0, 0)
            load(1, 1)
            with sp.Fori(0, blocks // 2 - 1) as i:
                for p in range(2):
                    sp.wait_ge(turned, 2 * (2 * i + p + 1))
                    load(2 * i + p + 2, p)
                    store(2 * i + p, p)
            store(blocks - 2, 0)
            store(blocks - 1, 1)
            for p in range(2):
                sp.wait_ge(stored[p], 16 * (blocks // 2 + 1))

        @block.gpsimd
        def _(pool):
            pool.iota(keys[:, :], [[-1, sparsity]], base=sparsity, channel_multiplier=0,
                      allow_small_or_imprecise_dtypes=True).then_inc(made, 1)
            pool.wait_ge(made, 1)
            pool.tensor_copy(key_bf[:, :], keys[:, :]).then_inc(made, 1)
            pool.sem_inc(stored[0], 16)
            pool.sem_inc(stored[1], 16)
            pool.sem_inc(h_out, tiles)
            pool.sem_inc(summed, tiles)
            pool.sem_inc(mask_out, 2)

        @block.tensor
        def _(pe):
            def turn_w(i, p, s):
                if s == 0:
                    pe.wait_ge(landed[p], 16 * (i + 1))
                for c in range(4):
                    last = pe.transpose(turn[:, s, c * P:(c + 1) * P], raw[p][:, (4 * s + c) * P:(4 * s + c + 1) * P],
                                        ident[:, :])
                last.then_inc(turned, 1)

            def gates(j, s):
                lo, n = parts[s]
                pe.sem_inc(waited, 1)
                for k in range(n):
                    last = pe.matmul(gate[:, k // 4, (k % 4) * P:(k % 4 + 1) * P],
                                     z[:, (lo + k) * P:(lo + k + 1) * P], c2_block(j), start=True, stop=True)
                last.then_inc(gated, 1)

            def c2_block(j):
                return c2t[:, bass.ds(j * P, P)]

            def turn_mask(j, p, s):
                lo, n = parts[s]
                pe.wait_ge(masked, 2 * j + s + 1)
                for k in range(n):
                    m = P if lo + k < tt - 1 else tail
                    last = pe.transpose(turn[:, s, :].bitcast(BF16)[:, k * P:k * P + m],
                                        mask[p][:m, (lo + k) * per:(lo + k + 1) * per, :].rearrange("q a b -> q (a b)"),
                                        ident_bf[:m, :m])
                last.then_inc(mask_turned, 1)

            def sums(j, p, t):
                pe.wait_ge(h_out, tiles * j + t + 1)
                product(pe, acc[:, t, :width], lambda a, c: w[p][:, a, c, :],
                        lambda a, c: x1t[:, a, c, t * width:(t + 1) * width], chunks).then_inc(summed, 1)

            def body(i, p, more):
                j = 2 * i + p
                pe.wait_ge(low, 2 * j + 2)
                sums(j, p, 0)
                if more:
                    pe.wait_ge(mask_out, 2 * j + 2)
                    turn_w(i + p, 1 - p, 0)
                sums(j, p, 1)
                if more:
                    turn_w(i + p, 1 - p, 1)
                    pe.wait_ge(compared, 2 * j + 2)
                    gates(j + 1, 0)
                    pe.wait_ge(low, 2 * j + 4)
                turn_mask(j, p, 0)
                turn_mask(j, p, 1)
                sums(j, p, 2)
                if more:
                    pe.wait_ge(compared, 2 * j + 3)
                    gates(j + 1, 1)
                sums(j, p, 3)

            turn_w(0, 0, 0)
            turn_w(0, 0, 1)
            gates(0, 0)
            pe.wait_ge(compared, 1)
            gates(0, 1)
            over_blocks(pe, body)

        @block.scalar
        def _(act):
            def high_part(j, p, s):
                act.wait_ge(turned, 2 * j + s + 1)
                act.activation(w[p][:, 0, 4 * s:4 * s + 4, :], turn[:, s, :].rearrange("q (c n) -> q c n", c=4),
                               ACT.Copy).then_inc(high, 1)

            def mask_part(j, s):
                lo, n = parts[s]
                a, e = lo * P, min((lo + n) * P, tokens)
                act.wait_ge(mask_turned, 2 * j + s + 1)
                act.wait_ge(h_out, tiles * (j + 1))
                act.activation(mask_t[:, a:e], turn[:, s, :].bitcast(BF16)[:, :e - a], ACT.Copy).then_inc(mask_out, 1)

            def body(i, p, more):
                j = 2 * i + p
                if more:
                    act.wait_ge(summed, tiles * (j + 1))
                    high_part(j + 1, 1 - p, 0)
                    high_part(j + 1, 1 - p, 1)
                mask_part(j, 0)
                mask_part(j, 1)

            high_part(0, 0, 0)
            high_part(0, 0, 1)
            over_blocks(act, body)

        @block.vector
        def _(dve):
            def low_part(j, p, s):
                dve.wait_ge(high, 2 * j + s + 1)
                dve.tensor_tensor(w[p][:, 1, 4 * s:4 * s + 4, :], turn[:, s, :].rearrange("q (c n) -> q c n", c=4),
                                  w[p][:, 0, 4 * s:4 * s + 4, :].bitcast(F32), ALU.subtract).then_inc(low, 1)

            def pick(j, p, s):
                lo, n = parts[s]
                g = n * per
                at = slice(lo * per, lo * per + g)
                k = STEPS * j + 4 * s
                values = gate[:, :, :].rearrange("q a (b c) -> q (a b) c", c=sparsity)[:, :g, :]
                dve.wait_ge(gated, 2 * j + s + 1)
                dve.tensor_reduce(top[:, at], values, AX.X, ALU.max).then_inc(step, 1)
                dve.wait_ge(step, k + 1)
                dve.tensor_tensor(equal[:, at, :], values, spread(top[:, at], g), ALU.is_equal).then_inc(compared, 1)
                dve.wait_ge(compared, 2 * j + s + 1)
                dve.tensor_tensor(equal[:, at, :], equal[:, at, :],
                                  key_bf[:, :].rearrange("q (a c) -> q a c", a=1).to_broadcast([P, g, sparsity]),
                                  ALU.mult).then_inc(step, 1)
                dve.wait_ge(step, k + 2)
                dve.tensor_reduce(lead[:, at], equal[:, at, :], AX.X, ALU.max).then_inc(step, 1)
                dve.wait_ge(step, k + 3)
                dve.tensor_tensor(mask[p][:, at, :], equal[:, at, :], spread(lead[:, at], g),
                                  ALU.is_equal).then_inc(masked, 1)
                dve.wait_ge(masked, 2 * j + s + 1)
                dve.sem_inc(step, 1)

            def spread(ap, g):
                return ap.rearrange("q (a c) -> q a c", c=1).to_broadcast([P, g, sparsity])

            def evacuate(i, p, t):
                j = 2 * i + p
                dve.wait_ge(summed, tiles * (j + 1) + t + 1)
                if t == 0:
                    dve.wait_ge(mask_out, 2 * j + 4)
                    dve.wait_ge(stored[p], 16 * (i + 1))
                at = slice(t * width, (t + 1) * width)
                dve.scalar_tensor_tensor(out=h[p][:, at], in0=acc[:, t, :width], scalar=0.0, in1=mask_t[:, at],
                                         op0=ALU.max, op1=ALU.mult).then_inc(h_out, 1)

            def body(i, p, more):
                j = 2 * i + p
                if more:
                    low_part(j + 1, 1 - p, 0)
                    low_part(j + 1, 1 - p, 1)
                    pick(j + 1, 1 - p, 0)
                evacuate(i, p, 0)
                evacuate(i, p, 1)
                if more:
                    pick(j + 1, 1 - p, 1)
                evacuate(i, p, 2)
                evacuate(i, p, 3)

            dve.wait_ge(made, 2)
            low_part(0, 0, 0)
            low_part(0, 0, 1)
            pick(0, 0, 0)
            pick(0, 0, 1)
            over_blocks(dve, body)


def project_out(nc, sem, name, left, weights, residual, out):
    chunks, _, tokens = left.shape
    cols = 512
    halves = weights.shape[1] // cols
    per = 4
    quads = chunks // per
    whole = tokens // P
    tail = tokens - whole * P
    tiles = whole + 1
    w_landed = [sem(f"{name}_w_landed{i}") for i in range(2)]
    l_landed = [sem(f"{name}_l_landed{i}") for i in range(2)]
    r_landed = [sem(f"{name}_r_landed{i}") for i in range(2)]
    stored = [sem(f"{name}_stored{i}") for i in range(2)]
    w_high, w_low = sem(name + "_w_high"), sem(name + "_w_low")
    l_high, l_low = sem(name + "_l_high"), sem(name + "_l_low")
    used, added, waited = sem(name + "_used"), sem(name + "_added"), sem(name + "_waited")
    assert whole % 2 == 0

    with ExitStack() as mem:
        def sb(n, shape, dt=F32):
            return mem.enter_context(nc.sbuf_tensor(f"{name}_{n}", shape, dt))

        w_raw = [sb(f"w_raw{i}", [P, per, cols]) for i in range(2)]
        w = sb("w", [P, 2, chunks, cols], F32R)
        l_raw = [sb(f"l_raw{i}", [P, per, P]) for i in range(2)]
        l = [sb(f"l{i}", [P, 2, per, P], F32R) for i in range(2)]
        res = [sb(f"res{i}", [P, cols]) for i in range(2)]
        y = [sb(f"y{i}", [P, cols]) for i in range(2)]
        acc = [mem.enter_context(nc.psum_tensor(f"{name}_acc{i}", [P, cols], F32)) for i in range(2)]
        block = mem.enter_context(nc.Block())
        left_v = left.rearrange("(q k) d t -> q d k t", k=per)
        w_v = weights.rearrange("(q k p) n -> q p k n", k=per, p=P)

        def over_tiles(eng, h, body):
            base = h * tiles
            body(0, base // 2, base % 2, P)
            with eng.Fori(0, (whole - 2) // 2) as i:
                for s in (1, 2):
                    body(2 * i + s, i + (base + s) // 2, (base + s) % 2, P)
            for last in (whole - 1, whole):
                body(last, (base + last) // 2, (base + last) % 2, P if last < whole else tail)

        @block.sync
        def _(sp):
            def rows_of(tt, h, rows):
                return bass.ds(tt * P, rows), slice(h * cols, (h + 1) * cols)

            def store(tt, h, i, p, rows):
                sp.wait_ge(added, 2 * i + p + 1 + 2)
                sp.sem_inc(waited, 1)
                sp.dma_start(out[rows_of(tt, h, rows)], y[p][:rows, :]).then_inc(stored[p], 16)

            for h in range(halves):
                def tile_loads(tt, i, p, rows):
                    n = 2 * i + p
                    sp.dma_start(res[p][:rows, :], residual[rows_of(tt, h, rows)]).then_inc(r_landed[p], 16)
                    for m in range(quads):
                        if isinstance(tt, int) and tt == 0:
                            sp.wait_ge(w_low, h * quads + m + 1)
                            sp.dma_start(w_raw[(h * quads + m) % 2][:, :, :],
                                         w_v[m, :, :, h * cols:(h + 1) * cols]).then_inc(w_landed[(h * quads + m) % 2], 16)
                        sp.wait_ge(l_low, n * quads + m + 1)
                        sp.sem_inc(waited, 1)
                        sp.dma_start(l_raw[(p * quads + m) % 2][:, :, :rows],
                                     left_v[m][:, :, bass.ds(tt * P, rows)]).then_inc(l_landed[(p * quads + m) % 2], 16)
                        if m == 3 and not (isinstance(i, int) and n == 0):
                            if isinstance(tt, int) and tt == 0:
                                store(whole, h - 1, i + p - 1, 1 - p, tail)
                            else:
                                store(tt - 1, h, i + p - 1, 1 - p, P)
                over_tiles(sp, h, tile_loads)
            store(whole, halves - 1, (halves * tiles - 1) // 2, (halves * tiles - 1) % 2, tail)
            for p in range(2):
                sp.wait_ge(stored[p], 16 * (1 + halves * tiles // 2))

        @block.gpsimd
        def _(pool):
            pool.sem_inc(w_low, 2)
            pool.sem_inc(l_low, 2)
            pool.sem_inc(used, 2)
            pool.sem_inc(added, 2)
            pool.sem_inc(stored[0], 16)
            pool.sem_inc(stored[1], 16)

        @block.scalar
        def _(act):
            for h in range(halves):
                def high_parts(tt, i, p, rows):
                    n = 2 * i + p
                    for m in range(quads):
                        j = p * quads + m
                        if isinstance(tt, int) and tt == 0:
                            g = h * quads + m
                            act.wait_ge(w_landed[g % 2], 16 * (g // 2 + 1))
                            if h:
                                act.wait_ge(used, 2 + ((tiles - 1) * quads + m + 1) + (h - 1) * tiles * quads)
                            act.activation(w[:, 0, m * per:(m + 1) * per], w_raw[g % 2][:, :, :],
                                           ACT.Copy).then_inc(w_high, 1)
                        act.wait_ge(l_landed[j % 2], 16 * (i * quads + j // 2 + 1))
                        act.wait_ge(used, n * quads + m + 1)
                        act.activation(l[j % 2][:, 0, :, :rows], l_raw[j % 2][:, :, :rows],
                                       ACT.Copy).then_inc(l_high, 1)
                over_tiles(act, h, high_parts)

        @block.vector
        def _(dve):
            def add(i, p, rows):
                dve.wait_ge(used, 2 + quads * (2 * i + p + 1))
                dve.wait_ge(r_landed[p], 16 * (i + 1))
                dve.wait_ge(stored[p], 16 * (i + 1))
                dve.tensor_tensor(y[p][:rows, :], acc[p][:rows, :], res[p][:rows, :], ALU.add).then_inc(added, 1)

            for h in range(halves):
                def low_parts(tt, i, p, rows):
                    n = 2 * i + p
                    for m in range(quads):
                        j = p * quads + m
                        if isinstance(tt, int) and tt == 0:
                            g = h * quads + m
                            dve.wait_ge(w_high, g + 1)
                            dve.tensor_tensor(w[:, 1, m * per:(m + 1) * per], w_raw[g % 2][:, :, :],
                                              w[:, 0, m * per:(m + 1) * per].bitcast(F32),
                                              ALU.subtract).then_inc(w_low, 1)
                        dve.wait_ge(l_high, n * quads + m + 1)
                        dve.tensor_tensor(l[j % 2][:, 1, :, :rows], l_raw[j % 2][:, :, :rows],
                                          l[j % 2][:, 0, :, :rows].bitcast(F32), ALU.subtract).then_inc(l_low, 1)
                        if m == 1 and not (isinstance(n, int) and n == 0):
                            before = tail if isinstance(tt, int) and tt == 0 else P
                            add(i + p - 1, 1 - p, before)
                over_tiles(dve, h, low_parts)
            add((halves * tiles - 1) // 2, (halves * tiles - 1) % 2, tail)

        @block.tensor
        def _(pe):
            for h in range(halves):
                def sums(tt, i, p, rows):
                    n = 2 * i + p
                    pe.wait_ge(added, n + 1)
                    for m in range(quads):
                        j = p * quads + m
                        if isinstance(tt, int) and tt == 0:
                            pe.wait_ge(w_low, h * quads + m + 1 + 2)
                        pe.wait_ge(l_low, n * quads + m + 1 + 2)
                        for k in range(per):
                            for a, c in PAIRS:
                                last = pe.matmul(acc[p][:rows, :], l[j % 2][:, a, k, :rows], w[:, c, m * per + k, :],
                                                 start=(m == 0 and k == 0 and (a, c) == PAIRS[0]),
                                                 stop=(m == quads - 1 and k == per - 1 and (a, c) == PAIRS[-1]))
                        last.then_inc(used, 1)
                over_tiles(pe, h, sums)


def cross_attention_and_sparse_ffn(nc, x, ctx, wq, wk, wv, wo, c1, c2, w1, w2t, out):
    batches, rows, hidden = x.shape
    chunks = hidden // P
    tokens = batches * rows
    d = P
    heads = wq.shape[1] // d
    groups = wk.shape[1] // d
    inter = w1.shape[0]
    rank = c1.shape[0]
    sparsity = 64
    padded = (tokens + P - 1) // P * P

    def scratch(name, shape, dt=F32):
        return nc.dram_tensor(name, shape, dt).ap()

    with ExitStack() as ctx_all:
        def sem(name):
            return ctx_all.enter_context(nc.semaphore(name))

        def sb(mem, name, shape, dt=F32):
            return mem.enter_context(nc.sbuf_tensor(name, shape, dt))

        q_dram = scratch("q_scratch", (batches, d, heads, rows))
        xt_dram = scratch("xt_scratch", (2, P, chunks, tokens))
        o_dram = scratch("o_scratch", (heads, d, tokens))
        x1_dram = scratch("x1_scratch", (batches, rows, hidden))
        h_dram = scratch("h_scratch", (inter // P, P, tokens))

        ident = sb(ctx_all, "ident", [P, P])
        ident_bf = sb(ctx_all, "ident_bf", [P, P], BF16)
        make_identity(nc, ident, ident_bf, sem("identity_made"))
        with ExitStack() as mem:
            wkv = sb(mem, "wkv", [P, 2, 2, chunks, wk.shape[1]], F32R)
            split_kv_weights(nc, sem, (wk, wv), wkv)
            with ExitStack() as mem_x:
                xt = sb(mem_x, "xt", [P, 2, chunks, tokens], F32R)
                normalise(nc, sem, "ln1", x, xt, ident)
                project_queries(nc, sem, wq, xt, q_dram, xt_dram, float(d) ** -0.5, batches, rows)
            attend(nc, sem, ctx, xt_dram, q_dram, wkv, o_dram, ident)
        project_out(nc, sem, "wo", o_dram, wo, x.rearrange("b r n -> (b r) n"),
                    x1_dram.rearrange("b r n -> (b r) n"))
        with ExitStack() as mem:
            x1t = sb(mem, "x1t", [P, 2, chunks, tokens], F32R)
            normalise(nc, sem, "ln2", x1_dram, x1t, ident)
            c2t = sb(mem, "c2t", [rank, inter])
            z = sb(mem, "z", [rank, padded])
            with ExitStack() as mem_c:
                c1t = sb(mem_c, "c1t", [P, 2, chunks, P], F32R)
                gate_weights(nc, sem, c1, c2, x1t, c1t, c2t, z, ident)
            hidden_layer(nc, sem, w1, x1t, c2t, z, h_dram, ident, ident_bf, sparsity)
        project_out(nc, sem, "w2", h_dram, w2t, x1_dram.rearrange("b r n -> (b r) n"),
                    out.rearrange("b r n -> (b r) n"))


_INS = ['x', 'ctx_4096', 'L0_xattn_Wq', 'L0_xattn_Wk', 'L0_xattn_Wv', 'L0_xattn_Wo',
        'L0_ffn_c1_w', 'L0_ffn_c2_w', 'L0_ffn_w1', 'L0_ffn_w2t']


def kernel(**inputs):
    import numpy as _np
    import concourse.bacc as _bacc
    from concourse import mybir as _mybir
    from concourse.bass_utils import run_bass_kernel_spmd as _run

    nc = _bacc.Bacc("TRN2", target_bir_lowering=False, num_devices=1)
    arrays, args = {}, []
    for name in _INS:
        a = _np.ascontiguousarray(inputs[name])
        arrays[f"in_{name}_dram"] = a
        args.append(nc.dram_tensor(f"in_{name}_dram", a.shape, _mybir.dt.from_np(a.dtype), kind="ExternalInput").ap())
    shape = inputs['x'].shape
    args.append(nc.dram_tensor("out_0_dram", shape, _mybir.dt.from_np(_np.dtype('float32')), kind="ExternalOutput").ap())
    cross_attention_and_sparse_ffn(nc, *args)
    r = _run(nc, [arrays], core_ids=[0])
    return r.results[0]["out_0_dram"]
```

```python
from contextlib import ExitStack

import concourse.bass as bass
from concourse import mybir

ALU = mybir.AluOpType
ACT = mybir.ActivationFunctionType
AX = mybir.AxisListType
F32 = mybir.dt.float32
F32R = mybir.dt.float32r
BF16 = mybir.dt.bfloat16

P = 128
EPS = 1e-5
PAIRS = ((0, 0), (0, 1), (1, 0))




def product(pe, out, left, right, chunks):
    for c in range(chunks):
        for a, b in PAIRS:
            last = pe.matmul(out, left(a, c), right(b, c),
                             start=(c == 0 and (a, b) == PAIRS[0]),
                             stop=(c == chunks - 1 and (a, b) == PAIRS[-1]))
    return last


def make_identity(nc, ident, ident_bf, made):
    with nc.Block() as block:
        @block.gpsimd
        def _(pool):
            pool.memset(ident[:, :], 0.0).then_inc(made, 1)
            pool.wait_ge(made, 1)
            pool.affine_select(out=ident[:, :], in_=ident[:, :], compare_op=ALU.not_equal, fill=1.0,
                               base=0, pattern=[[-1, P]], channel_multiplier=1).then_inc(made, 1)
            pool.wait_ge(made, 2)
            pool.tensor_copy(ident_bf[:, :], ident[:, :]).then_inc(made, 1)


def split_kv_weights(nc, sem, sources, wkv):
    landed = [sem("key_weights_landed"), sem("value_weights_landed")]
    high, low = sem("kvw_high"), sem("kvw_low")
    chunks, width = wkv.shape[3], wkv.shape[4]
    with ExitStack() as mem:
        raw = mem.enter_context(nc.sbuf_tensor("kvw_raw", [P, 2, chunks, width], F32))
        block = mem.enter_context(nc.Block())

        @block.sync
        def _(sp):
            for w, source in enumerate(sources):
                sp.dma_start(raw[:, w], source.rearrange("(c p) n -> p c n", p=P)).then_inc(landed[w], 16)

        @block.scalar
        def _(act):
            for w in range(2):
                act.wait_ge(landed[w], 16)
                act.activation(wkv[:, w, 0], raw[:, w], ACT.Copy).then_inc(high, 1)

        @block.vector
        def _(dve):
            for w in range(2):
                dve.wait_ge(high, w + 1)
                dve.tensor_tensor(wkv[:, w, 1], raw[:, w], wkv[:, w, 0].bitcast(F32),
                                  ALU.subtract).then_inc(low, 1)


def normalise(nc, sem, name, source, xt, ident):
    batches, rows, hidden = source.shape
    chunks = hidden // P
    half = hidden // 2
    landed, used = [sem(f"{name}_landed{i}") for i in range(2)], sem(name + "_used")
    step, rooted = sem(name + "_step"), sem(name + "_rooted")
    ready, turned = sem(name + "_ready"), sem(name + "_turned")
    high, low = sem(name + "_high"), sem(name + "_low")
    waited = sem(name + "_waited")
    STEPS = 7

    with ExitStack() as mem:
        def sb(n, shape, dt=F32):
            return mem.enter_context(nc.sbuf_tensor(f"{name}_{n}", shape, dt))

        raw = [sb(f"raw{i}", [P, hidden]) for i in range(2)]
        xn = [sb(f"xn{i}", [P, hidden]) for i in range(2)]
        stats = [sb(f"stats{i}", [P, 2, 6]) for i in range(2)]
        moments = [sb(f"moments{i}", [P, 2]) for i in range(2)]
        small = [sb(f"small{i}", [P, 6]) for i in range(2)]
        turned_ps = [mem.enter_context(nc.psum_tensor(f"{name}_ps{i}", [P, chunks, P], F32)) for i in range(2)]
        block = mem.enter_context(nc.Block())

        @block.sync
        def _(sp):
            for b in range(2):
                sp.dma_start(raw[b][:rows, :], source[b]).then_inc(landed[b], 16)
            with sp.Fori(0, batches // 2 - 1) as i:
                for b in range(2):
                    sp.wait_ge(used, 2 * i + b + 1)
                    sp.dma_start(raw[b][:rows, :],
                                 source[bass.ds(2 * i + b + 2, 1)].rearrange("a r n -> (a r) n")).then_inc(landed[b], 16)

        @block.vector
        def _(dve):
            def norm(k, p):
                b = 2 * k + p
                v, m, s = small[p], moments[p], stats[p]
                dve.wait_ge(landed[p], 16 * (k + 1))
                for c in range(2):
                    last = dve.bn_stats(s[:rows, c, :], raw[p][:rows, c * half:(c + 1) * half])
                last.then_inc(step, 1)
                dve.wait_ge(step, STEPS * b + 1)
                dve.sem_inc(waited, 1)
                dve.bn_aggr(m[:rows, :], s[:rows, :, :]).then_inc(step, 1)
                dve.wait_ge(step, STEPS * b + 2)
                dve.tensor_scalar(v[:rows, 0:1], m[:rows, 1:2], EPS, None, ALU.add).then_inc(step, 1)
                dve.wait_ge(rooted, b + 1)
                dve.reciprocal(v[:rows, 2:3], v[:rows, 1:2]).then_inc(step, 1)
                dve.wait_ge(step, STEPS * b + 4)
                dve.scalar_tensor_tensor(out=v[:rows, 3:4], in0=v[:rows, 2:3], scalar=v[:rows, 2:3],
                                         in1=v[:rows, 0:1], op0=ALU.mult, op1=ALU.mult).then_inc(step, 1)
                dve.wait_ge(step, STEPS * b + 5)
                dve.tensor_scalar(v[:rows, 4:5], v[:rows, 3:4], -0.5, 1.5, ALU.mult, ALU.add).then_inc(step, 1)
                dve.wait_ge(step, STEPS * b + 6)
                dve.tensor_tensor(v[:rows, 5:6], v[:rows, 2:3], v[:rows, 4:5], ALU.mult).then_inc(step, 1)
                dve.wait_ge(step, STEPS * b + 7)
                dve.tensor_scalar(xn[p][:rows, :], raw[p][:rows, :], m[:rows, 0:1], v[:rows, 5:6],
                                  ALU.subtract, ALU.mult).then_inc(ready, 1)

            def low_part(b, p):
                dve.wait_ge(high, b + 1)
                at = slice(b * rows, b * rows + rows) if isinstance(b, int) else bass.ds(b * rows, rows)
                dve.tensor_tensor(xt[:, 1, :, at], turned_ps[p][:, :, :rows], xt[:, 0, :, at].bitcast(F32),
                                  ALU.subtract).then_inc(low, 1)

            norm(0, 0)
            with dve.Fori(0, batches // 2 - 1) as i:
                norm(i, 1)
                low_part(2 * i, 0)
                norm(i + 1, 0)
                low_part(2 * i + 1, 1)
            norm(batches // 2 - 1, 1)
            low_part(batches - 2, 0)
            low_part(batches - 1, 1)

        @block.gpsimd
        def _(pool):
            with pool.Fori(0, batches) as i:
                pool.wait_ge(ready, i + 1)
                pool.sem_inc(used, 1)

        @block.scalar
        def _(act):
            def root(b, p):
                act.wait_ge(step, STEPS * b + 3)
                act.activation(small[p][:rows, 1:2], small[p][:rows, 0:1], ACT.Sqrt).then_inc(rooted, 1)

            def high_part(b, p):
                act.wait_ge(turned, b + 1)
                at = slice(b * rows, b * rows + rows) if isinstance(b, int) else bass.ds(b * rows, rows)
                act.activation(xt[:, 0, :, at], turned_ps[p][:, :, :rows], ACT.Copy).then_inc(high, 1)

            root(0, 0)
            with act.Fori(0, batches // 2 - 1) as i:
                root(2 * i + 1, 1)
                high_part(2 * i, 0)
                root(2 * i + 2, 0)
                high_part(2 * i + 1, 1)
            root(batches - 1, 1)
            high_part(batches - 2, 0)
            high_part(batches - 1, 1)

        @block.tensor
        def _(pe):
            def turn(b, p):
                pe.wait_ge(ready, b + 1)
                for c in range(chunks):
                    last = pe.transpose(turned_ps[p][:, c, :rows], xn[p][:rows, c * P:(c + 1) * P],
                                        ident[:rows, :rows])
                last.then_inc(turned, 1)

            turn(0, 0)
            turn(1, 1)
            with pe.Fori(0, batches // 2 - 1) as i:
                for p in range(2):
                    pe.wait_ge(low, 2 * i + p + 1)
                    turn(2 * i + p + 2, p)


def project_queries(nc, sem, wq, xt, q_dram, xt_dram, scale, batches, rows):
    hidden = wq.shape[0]
    chunks = hidden // P
    heads = q_dram.shape[2]
    tokens = batches * rows
    tiles, width = 4, tokens // 4
    landed = [sem(f"wq_landed{i}") for i in range(2)]
    high, low = sem("wq_high"), sem("wq_low")
    summed = sem("q_summed")
    out_act, out_dve = sem("q_out_act"), sem("q_out_dve")
    stage_free, saved = [sem(f"q_stage_free{i}") for i in range(2)], sem("xt_saved")

    with ExitStack() as mem:
        def sb(n, shape, dt=F32):
            return mem.enter_context(nc.sbuf_tensor(n, shape, dt))

        raw = [sb(f"wq_raw{i}", [P, chunks, P]) for i in range(2)]
        w = [sb(f"wq_parts{i}", [P, 2, chunks, P], F32R) for i in range(2)]
        stage = [sb(f"q_stage{i}", [P, tokens]) for i in range(2)]
        acc = mem.enter_context(nc.psum_tensor("q_acc", [P, 2, tiles, 512], F32))
        block = mem.enter_context(nc.Block())
        wq_v = wq.rearrange("(c p) n -> p c n", p=P)
        q_v = q_dram.rearrange("b d h r -> h d b r")

        @block.sync
        def _(sp):
            def load(h, p):
                at = slice(h * P, (h + 1) * P) if isinstance(h, int) else bass.ds(h * P, P)
                sp.dma_start(raw[p][:, :, :], wq_v[:, :, at]).then_inc(landed[p], 16)

            def store(h, p):
                sp.wait_ge(out_act, 2 * h + 2 + 4)
                sp.wait_ge(out_dve, 2 * h + 2 + 4)
                sp.dma_start(q_v[bass.ds(h, 1)].rearrange("a d b r -> (a d) b r"),
                             stage[p][:, :].rearrange("p (b r) -> p b r", b=batches)).then_inc(stage_free[p], 16)

            load(0, 0)
            load(1, 1)
            for part in range(2):
                sp.dma_start(xt_dram[part], xt[:, part].bitcast(F32)).then_inc(saved, 16)
            with sp.Fori(0, heads // 2 - 1) as i:
                for p in range(2):
                    sp.wait_ge(low, 2 * i + p + 1)
                    load(2 * i + p + 2, p)
                    store(2 * i + p, p)
            store(heads - 2, 0)
            store(heads - 1, 1)
            for p in range(2):
                sp.wait_ge(stage_free[p], 16 * (heads // 2 + 1))
            sp.wait_ge(saved, 32)

        @block.gpsimd
        def _(pool):
            pool.sem_inc(stage_free[0], 16)
            pool.sem_inc(stage_free[1], 16)
            pool.sem_inc(out_act, 4)
            pool.sem_inc(out_dve, 4)

        @block.scalar
        def _(act):
            def split(k, p):
                act.wait_ge(landed[p], 16 * (k + 1))
                act.activation(w[p][:, 0], raw[p][:, :, :], ACT.Copy).then_inc(high, 1)

            def evacuate(k, p):
                h = 2 * k + p
                act.wait_ge(stage_free[p], 16 * (k + 1))
                for t in (0, 2):
                    act.wait_ge(summed, tiles * h + t + 1)
                    act.activation(stage[p][:, t * width:(t + 1) * width], acc[:, p, t, :width], ACT.Copy,
                                   scale=scale).then_inc(out_act, 1)

            split(0, 0)
            split(0, 1)
            with act.Fori(0, heads // 2 - 1) as i:
                for p in range(2):
                    evacuate(i, p)
                    act.wait_ge(summed, tiles * (2 * i + p + 1))
                    split(i + 1, p)
            evacuate(heads // 2 - 1, 0)
            evacuate(heads // 2 - 1, 1)

        @block.vector
        def _(dve):
            def split(k, p):
                dve.wait_ge(high, 2 * k + p + 1)
                dve.tensor_tensor(w[p][:, 1], raw[p][:, :, :], w[p][:, 0].bitcast(F32),
                                  ALU.subtract).then_inc(low, 1)

            def evacuate(k, p):
                h = 2 * k + p
                dve.wait_ge(stage_free[p], 16 * (k + 1))
                for t in (1, 3):
                    dve.wait_ge(summed, tiles * h + t + 1)
                    dve.tensor_scalar(stage[p][:, t * width:(t + 1) * width], acc[:, p, t, :width], scale, None,
                                      ALU.mult).then_inc(out_dve, 1)

            split(0, 0)
            split(0, 1)
            with dve.Fori(0, heads // 2 - 1) as i:
                for p in range(2):
                    evacuate(i, p)
                    split(i + 1, p)
            evacuate(heads // 2 - 1, 0)
            evacuate(heads // 2 - 1, 1)

        @block.tensor
        def _(pe):
            with pe.Fori(0, heads // 2) as i:
                for p in range(2):
                    h = 2 * i + p
                    pe.wait_ge(low, h + 1)
                    for t in range(tiles):
                        pe.wait_ge(out_act if t % 2 == 0 else out_dve, 2 * h + t // 2 + 1)
                        product(pe, acc[:, p, t, :width], lambda a, c: w[p][:, a, c, :],
                                lambda a, c: xt[:, a, c, t * width:(t + 1) * width], chunks).then_inc(summed, 1)


def attend(nc, sem, ctx, xt_dram, q_dram, wkv, o_dram, ident):
    batches, keys_ctx, hidden = ctx.shape
    _, d, heads, rows = q_dram.shape
    groups = wkv.shape[4] // d
    per = heads // groups
    chunks = hidden // P
    kv = keys_ctx + rows
    kvp = kv + kv % 2
    row_chunks = [(c * P, min(P, keys_ctx - c * P)) for c in range((keys_ctx + P - 1) // P)]
    kv_chunks = [(c * P, min(P, kv - c * P)) for c in range((kv + P - 1) // P)]
    NC = len(kv_chunks)
    full = keys_ctx // P
    cols = per * rows
    half = cols // 2
    tile = 116
    tiles = [(t * tile, min(tile, cols - t * tile)) for t in range((cols + tile - 1) // tile)]
    NT = len(tiles)
    N = groups * NT
    SB, TB, OB, KB, RB, LAG = 2, 2, 2, 2, 4, 3
    FIRST = chunks + groups
    USES = NC + chunks + groups
    half_at = [max(t for t, (a, _) in enumerate(tiles) if a < half) + 1, NT]
    STEPS = N + LAG + 4
    PARTS = 3

    def portion(count, steps, s):
        return range(count * s // steps, count * (s + 1) // steps)

    V_STEPS, T_FIRST, K_FIRST, K_STEPS = 6, 7, 8 + chunks, 4
    products = chunks * len(PAIRS)

    def v_work(i):
        return portion(NC * products, V_STEPS, i) if i < V_STEPS else ()

    def k_work(i):
        if i < K_FIRST:
            return 0, ()
        g = min((i - K_FIRST) // K_STEPS, groups - 1)
        steps = K_STEPS if g < groups - 1 else STEPS - K_FIRST - K_STEPS * (groups - 1)
        return g, portion(products, steps, i - K_FIRST - K_STEPS * g)

    def ended(i, more):
        out = [x // products for x in v_work(i) if x % products == products - 1]
        if more:
            if 0 <= i - T_FIRST < chunks:
                out.append(NC + i - T_FIRST)
            g, pieces = k_work(i)
            if products - 1 in pieces:
                out.append(NC + chunks + g)
        return out

    assert NC * P <= 512 and tile * NC <= 512 and FIRST % KB == 0 and USES % KB == 0 and N % RB == 0
    ctx_landed, lat_landed = sem("ctx_landed"), sem("lat_landed")
    q_landed = [sem(f"q_landed{i}") for i in range(2)]
    kv_full, kv_high, kv_free = sem("kv_full"), sem("kv_high"), sem("kv_free")
    q_high, q_split = sem("q_high"), sem("q_split")
    s_full, s_max, exped = sem("s_full"), sem("s_max"), sem("exped")
    inverted, scaled = sem("inverted"), sem("scaled")
    pt_full, pt_high, pt_low = sem("pt_full"), sem("pt_high"), sem("pt_low")
    o_full, o_out = sem("o_full"), sem("o_out")
    o_free = [sem(f"o_free{i}") for i in range(2)]
    cleared, waited = sem("attend_cleared"), sem("attend_waited")

    with ExitStack() as mem:
        def sb(n, shape, dt=F32):
            return mem.enter_context(nc.sbuf_tensor(n, shape, dt))

        ctx_raw = sb("ctx_raw", [P, len(row_chunks), hidden])
        hst = sb("hst", [P, 2, chunks, kvp], F32R)
        kt = sb("kt", [P, 2, groups, kvp], F32R)
        v = sb("v", [P, 2, NC, groups * P], F32R)
        q_raw = [sb(f"q_raw{i}", [P, cols]) for i in range(2)]
        q = [sb(f"q_parts{i}", [P, 2, cols], F32R) for i in range(2)]
        probs = sb("probs", [P, RB, NC * P])
        pt = sb("pt", [P, 2, NC, cols], F32R)
        o = [sb(f"o_stage{i}", [P, cols]) for i in range(2)]
        negmax = sb("negmax", [P, RB])
        total = sb("total", [P, RB])
        inverse = sb("inverse", [P, RB])
        scores = mem.enter_context(nc.psum_tensor("scores", [P, SB, 512], F32))
        turned = mem.enter_context(nc.psum_tensor("turned", [P, TB, 512], F32))
        outs = mem.enter_context(nc.psum_tensor("outs", [P, OB, 512], F32))
        kvb = mem.enter_context(nc.psum_tensor("kvb", [P, KB, 512], F32))
        block = mem.enter_context(nc.Block())
        q_v = q_dram.rearrange("b d (g h) r -> g b d (h r)", g=groups)
        o_v = o_dram.rearrange("(g h) d (b r) -> g b d h r", g=groups, b=batches)

        def bank_of(u):
            if u >= NC + chunks:
                return kvb[:, u % KB, :kvp]
            if u >= NC:
                return kvb[:, u % KB, :keys_ctx]
            return kvb[:kv_chunks[u][1], u % KB, :]

        def part_of(u, part, dt):
            if u >= NC + chunks:
                return kt[:, part, u - NC - chunks, :].bitcast(dt)
            if u >= NC:
                return hst[:, part, u - NC, :keys_ctx].bitcast(dt)
            return v[:kv_chunks[u][1], part, u, :].bitcast(dt)

        def turned_tile(i, n):
            return turned[:, i % TB, :NC * tile].rearrange("p (k n) -> p k n", k=NC)[:, :, :n]

        @block.sync
        def _(sp):
            def load_ctx(b):
                rows_b = ctx[bass.ds(b, 1)].rearrange("a r n -> (a r) n")
                sp.dma_start(ctx_raw[:, :full, :],
                             rows_b[:full * P, :].rearrange("(c p) n -> p c n", p=P)).then_inc(ctx_landed, 16)
                sp.dma_start(ctx_raw[:keys_ctx - full * P, full, :], rows_b[full * P:, :]).then_inc(ctx_landed, 16)

            def load_latents(b):
                for part in range(2):
                    sp.dma_start(hst[:, part, :, keys_ctx:kv].bitcast(F32),
                                 xt_dram[part, :, :, bass.ds(b * rows, rows)]).then_inc(lat_landed, 16)

            def load_q(b, g):
                sp.dma_start(q_raw[g % 2][:, :],
                             q_v[g, bass.ds(b, 1)].rearrange("a d n -> (a d) n")).then_inc(q_landed[g % 2], 16)

            def store_o(b, g):
                sp.wait_ge(o_out, 2 * (groups * b + g + 1) + OB)
                sp.dma_start(o_v[g, bass.ds(b, 1)].rearrange("a d h r -> (a d) h r"),
                             o[g % 2][:, :].rearrange("p (h r) -> p h r", h=per)).then_inc(o_free[g % 2], 16)

            def batch(b, more):
                if more:
                    sp.wait_ge(kv_full, USES * b + chunks)
                    load_ctx(b + 1)
                for g in range(groups):
                    if g + 2 < groups or more:
                        sp.wait_ge(q_split, 2 * (groups * b + g + 1))
                        if g + 2 < groups:
                            load_q(b, g + 2)
                        else:
                            load_q(b + 1, g + 2 - groups)
                    if g == 1 and more:
                        sp.wait_ge(kv_full, FIRST + USES * b + NC)
                        load_latents(b + 1)
                    if g >= 2:
                        store_o(b, g - 2)
                store_o(b, groups - 2)
                store_o(b, groups - 1)

            load_ctx(0)
            load_latents(0)
            load_q(0, 0)
            load_q(0, 1)
            with sp.Fori(0, batches - 1) as b:
                batch(b, True)
            batch(batches - 1, False)
            for p in range(2):
                sp.wait_ge(o_free[p], 16 * (1 + groups // 2 * batches))

        @block.gpsimd
        def _(pool):
            pool.memset(hst[:, :, :, kv:].bitcast(F32), 0.0).then_inc(cleared, 1)
            pool.memset(probs[:, :, :], 0.0).then_inc(cleared, 1)
            pool.sem_inc(kv_free, KB)
            pool.sem_inc(o_out, OB)
            pool.sem_inc(o_free[0], 16)
            pool.sem_inc(o_free[1], 16)

            def split_q(b, g, part, h):
                at = slice(h * half, (h + 1) * half)
                if part == 0 and h == 0:
                    pool.wait_ge(q_landed[g % 2], 16 * (groups // 2 * b + g // 2 + 1))
                    pool.sem_inc(waited, 1)
                if part == 0:
                    pool.tensor_scalar(q[g % 2][:, 0, at], q_raw[g % 2][:, at], 1.0, 1.0,
                                       ALU.mult, ALU.mult).then_inc(q_high, 1)
                else:
                    pool.wait_ge(q_high, 2 * (groups * b + g) + h + 1)
                    pool.tensor_tensor(q[g % 2][:, 1, at], q_raw[g % 2][:, at], q[g % 2][:, 0, at].bitcast(F32),
                                       ALU.subtract).then_inc(q_split, 1)

            def batch(b, more):
                for i in range(N):
                    g, t = divmod(i, NT)
                    n = tiles[t][1]
                    pool.wait_ge(inverted, N * b + i + 1)
                    pool.sem_inc(waited, 1)
                    pool.tensor_scalar(probs[:n, i % RB, :kv], probs[:n, i % RB, :kv], inverse[:n, i % RB:i % RB + 1],
                                       1.0, ALU.mult, ALU.mult).then_inc(scaled, 1)
                    if 1 <= t < 5:
                        piece = ((t - 1) % 2, (t - 1) // 2)
                        if g + 1 < groups:
                            split_q(b, g + 1, *piece)
                        elif more:
                            split_q(b + 1, 0, *piece)

            for h in range(2):
                for part in range(2):
                    split_q(0, 0, part, h)
            with pool.Fori(0, batches - 1) as b:
                batch(b, True)
            batch(batches - 1, False)

        @block.tensor
        def _(pe):
            def take(b, u):
                pe.wait_ge(kv_free, FIRST + USES * b + u + 1)

            def turn_ctx(c):
                u = NC + c
                for r, (a, n) in enumerate(row_chunks):
                    last = pe.transpose(kvb[:, u % KB, a:a + n], ctx_raw[:n, r, c * P:(c + 1) * P], ident[:n, :n])
                last.then_inc(kv_full, 1)

            def sum_keys(b, g, pieces):
                u = NC + chunks + g
                for x in pieces:
                    c, (a, e) = x // len(PAIRS), PAIRS[x % len(PAIRS)]
                    if x == 0:
                        take(b, u)
                    mm = pe.matmul(kvb[:, u % KB, :kvp], wkv[:, 0, a, c, g * P:(g + 1) * P], hst[:, e, c, :],
                                   start=(x == 0), stop=(x == products - 1))
                    if x == products - 1:
                        mm.then_inc(kv_full, 1)

            def sum_values(b, pieces):
                for y in pieces:
                    k, x = divmod(y, products)
                    at, n = kv_chunks[k]
                    c, (a, e) = x // len(PAIRS), PAIRS[x % len(PAIRS)]
                    if x == 0:
                        take(b, k)
                    mm = pe.matmul(kvb[:n, k % KB, :], hst[:, a, c, at:at + n], wkv[:, 1, e, c, :],
                                   start=(x == 0), stop=(x == products - 1))
                    if x == products - 1:
                        mm.then_inc(kv_full, 1)

            def score(b, i):
                g, t = divmod(i, NT)
                at, n = tiles[t]
                if t == 0:
                    pe.wait_ge(q_split, 2 * (groups * b + g + 1))
                if i >= SB:
                    pe.wait_ge(exped, N * b + i - SB + 1)
                product(pe, scores[:n, i % SB, :kvp], lambda a, c: q[g % 2][:, a, at:at + n],
                        lambda a, c: kt[:, a, g, :], 1).then_inc(s_full, 1)

            def turn(b, i):
                n = tiles[i % NT][1]
                pe.wait_ge(scaled, N * b + i + 1)
                if i >= TB:
                    pe.wait_ge(pt_low, N * b + i - TB + 1)
                for k in range(NC):
                    last = pe.transpose(turned[:, i % TB, k * tile:k * tile + n],
                                        probs[:n, i % RB, k * P:(k + 1) * P], ident[:n, :n])
                last.then_inc(pt_full, 1)

            def weigh(b, g, h, s):
                for x in portion(NC * len(PAIRS), PARTS, s):
                    k, (a, e) = x // len(PAIRS), PAIRS[x % len(PAIRS)]
                    n = kv_chunks[k][1]
                    if x == 0:
                        pe.wait_ge(pt_low, N * b + NT * g + half_at[h])
                        pe.wait_ge(o_out, 2 * (groups * b + g) + h + 1)
                    mm = pe.matmul(outs[:, h, :half], v[:n, a, k, g * P:(g + 1) * P],
                                   pt[:n, e, k, h * half:(h + 1) * half],
                                   start=(x == 0), stop=(x == NC * len(PAIRS) - 1))
                mm_last = x == NC * len(PAIRS) - 1
                if mm_last:
                    mm.then_inc(o_full, 1)

            def batch(b, more):
                for i in range(STEPS):
                    if i < N:
                        score(b, i)
                    j = i - LAG
                    for g in range(groups):
                        for h in range(2):
                            s = j - (NT * g + half_at[h] + 1)
                            if 0 <= s < PARTS:
                                if g == 0 and h == 0 and s == 0:
                                    pe.wait_ge(kv_free, FIRST + USES * b + NC + KB)
                                weigh(b, g, h, s)
                    if 0 <= j < N:
                        turn(b, j)
                    sum_values(b, v_work(i))
                    if more and 0 <= i - T_FIRST < chunks:
                        if i == T_FIRST:
                            pe.wait_ge(ctx_landed, 32 * (b + 2))
                        take(b, NC + i - T_FIRST)
                        turn_ctx(i - T_FIRST)
                    if more:
                        g, pieces = k_work(i)
                        if i == K_FIRST:
                            pe.wait_ge(kv_free, FIRST + USES * b + NC + chunks + KB)
                            pe.wait_ge(lat_landed, 32 * (b + 2))
                        sum_keys(b, g, pieces)

            pe.wait_ge(cleared, 2)
            pe.wait_ge(ctx_landed, 32)
            for c in range(chunks):
                take(-1, NC + c)
                turn_ctx(c)
            pe.wait_ge(lat_landed, 32)
            pe.wait_ge(kv_free, chunks + KB)
            for g in range(groups):
                sum_keys(-1, g, range(products))
            pe.wait_ge(kv_free, FIRST + KB)
            with pe.Fori(0, batches - 1) as b:
                batch(b, True)
            batch(batches - 1, False)

        @block.scalar
        def _(act):
            def high_part(b, u):
                act.wait_ge(kv_full, FIRST + USES * b + u + 1)
                act.activation(part_of(u, 0, F32R), bank_of(u), ACT.Copy).then_inc(kv_high, 1)

            def batch(b, more):
                for i in range(STEPS + 1):
                    j = i - LAG
                    if 0 <= j < N:
                        at, n = tiles[j % NT]
                        act.wait_ge(pt_full, N * b + j + 1)
                        act.activation(pt[:, 0, :, at:at + n], turned_tile(j, n), ACT.Copy).then_inc(pt_high, 1)
                    if i < N:
                        n = tiles[i % NT][1]
                        act.wait_ge(s_max, N * b + i + 1)
                        if i >= RB:
                            act.wait_ge(pt_full, N * b + i - RB + 1)
                        act.activation(probs[:n, i % RB, :kv], scores[:n, i % SB, :kv], ACT.Exp,
                                       bias=negmax[:n, i % RB:i % RB + 1],
                                       accum_out=total[:n, i % RB:i % RB + 1]).then_inc(exped, 1)
                    if i >= 1:
                        for u in ended(i - 1, more):
                            high_part(b, u)

            for u in range(NC, USES):
                high_part(-1, u)
            with act.Fori(0, batches - 1) as b:
                batch(b, True)
            batch(batches - 1, False)

        @block.vector
        def _(dve):
            def low_part(b, u):
                dve.wait_ge(kv_high, FIRST + USES * b + u + 1)
                dve.tensor_tensor(part_of(u, 1, F32R), bank_of(u), part_of(u, 0, F32),
                                  ALU.subtract).then_inc(kv_free, 1)

            def batch(b, more):
                for i in range(STEPS + 1):
                    if i < N:
                        n = tiles[i % NT][1]
                        dve.wait_ge(s_full, N * b + i + 1)
                        if i >= RB:
                            dve.wait_ge(exped, N * b + i - RB + 1)
                        dve.tensor_reduce(negmax[:n, i % RB:i % RB + 1], scores[:n, i % SB, :kv], AX.X, ALU.max,
                                          negate=True).then_inc(s_max, 1)
                    if 1 <= i < N + 1:
                        j = i - 1
                        n = tiles[j % NT][1]
                        dve.wait_ge(exped, N * b + j + 1)
                        if j >= RB:
                            dve.wait_ge(scaled, N * b + j - RB + 1)
                        dve.reciprocal(inverse[:n, j % RB:j % RB + 1],
                                       total[:n, j % RB:j % RB + 1]).then_inc(inverted, 1)
                    j = i - LAG
                    if 0 <= j < N:
                        at, n = tiles[j % NT]
                        dve.wait_ge(pt_high, N * b + j + 1)
                        dve.tensor_tensor(pt[:, 1, :, at:at + n], turned_tile(j, n),
                                          pt[:, 0, :, at:at + n].bitcast(F32), ALU.subtract).then_inc(pt_low, 1)
                    for g in range(groups):
                        for h in range(2):
                            if j == NT * g + half_at[h] + PARTS:
                                dve.wait_ge(o_full, 2 * (groups * b + g) + h + 1)
                                if h == 0:
                                    dve.wait_ge(o_free[g % 2], 16 * (groups // 2 * b + g // 2 + 1))
                                dve.tensor_copy(o[g % 2][:, h * half:(h + 1) * half],
                                                outs[:, h, :half]).then_inc(o_out, 1)
                    if i >= 1:
                        for u in ended(i - 1, more):
                            low_part(b, u)

            for u in range(NC, USES):
                low_part(-1, u)
            with dve.Fori(0, batches - 1) as b:
                batch(b, True)
            batch(batches - 1, False)


def gate_weights(nc, sem, c1, c2, x1t, c1t, c2s, zs, ident):
    rank, hidden = c1.shape
    inter = c2.shape[0]
    chunks, blocks = hidden // P, inter // P
    starts = (0, 32, 64)
    K = starts[-1] + rank
    tokens = x1t.shape[3]
    width = tokens // 4
    per = 4
    rounds = blocks // per
    cleared, landed = sem("gate_cleared"), sem("gate_landed")
    full, high, done = sem("gate_full"), sem("gate_high"), sem("gate_done")
    with ExitStack() as mem:
        c1_raw = mem.enter_context(nc.sbuf_tensor("c1_raw", [P, hidden], F32))
        c2_raw = mem.enter_context(nc.sbuf_tensor("c2_raw", [P, blocks, P], F32))
        banks = mem.enter_context(nc.psum_tensor("gate_banks", [P, 8, 512], F32))
        block = mem.enter_context(nc.Block())

        @block.gpsimd
        def _(pool):
            pool.memset(c1_raw[:, :], 0.0).then_inc(cleared, 1)
            pool.memset(c2_raw[:, :, :], 0.0).then_inc(cleared, 1)
            pool.memset(zs[:, :].bitcast(F32), 0.0).then_inc(cleared, 1)

        @block.sync
        def _(sp):
            sp.wait_ge(cleared, 2)
            for s in starts:
                sp.dma_start(c1_raw[s:s + rank, :], c1).then_inc(landed, 16)
                sp.dma_start(c2_raw[:, :, s:s + rank], c2.rearrange("(j p) r -> p j r", p=P)).then_inc(landed, 16)

        @block.tensor
        def _(pe):
            pe.wait_ge(landed, 32 * len(starts))
            for h in range(2):
                for c in range(4):
                    last = pe.transpose(banks[:, h, c * P:(c + 1) * P],
                                        c1_raw[:, (4 * h + c) * P:(4 * h + c + 1) * P], ident[:, :])
                last.then_inc(full, 1)
            for r in range(rounds):
                if 2 + r >= 8:
                    pe.wait_ge(done, r - 5)
                for k in range(per):
                    last = pe.transpose(banks[:, (2 + r) % 8, k * P:(k + 1) * P], c2_raw[:, per * r + k, :], ident[:, :])
                last.then_inc(full, 1)
            for t in range(4):
                pe.wait_ge(done, 2 + t)
                product(pe, banks[:, 1 + t, :width], lambda a, c: c1t[:, a, c, :],
                        lambda a, c: x1t[:, a, c, t * width:(t + 1) * width], chunks).then_inc(full, 1)

        @block.scalar
        def _(act):
            for h in range(2):
                act.wait_ge(full, h + 1)
                act.activation(c1t[:, 0, 4 * h:4 * h + 4, :], banks[:, h, :].rearrange("p (c n) -> p c n", c=4),
                               ACT.Copy).then_inc(high, 1)
            for r in range(rounds):
                act.wait_ge(full, 3 + r)
                act.activation(c2s[:, r * 512:(r + 1) * 512], banks[:K, (2 + r) % 8, :], ACT.Copy).then_inc(high, 1)
            act.wait_ge(cleared, 3)
            for t in range(4):
                act.wait_ge(full, 3 + rounds + t)
                act.activation(zs[:, t * width:(t + 1) * width], banks[:K, 1 + t, :width], ACT.Copy).then_inc(high, 1)

        @block.vector
        def _(dve):
            for h in range(2):
                dve.wait_ge(high, h + 1)
                dve.tensor_tensor(c1t[:, 1, 4 * h:4 * h + 4, :], banks[:, h, :].rearrange("p (c n) -> p c n", c=4),
                                  c1t[:, 0, 4 * h:4 * h + 4, :].bitcast(F32), ALU.subtract).then_inc(done, 1)
            for r in range(rounds):
                low = slice(starts[1], starts[1] + rank)
                at = slice(r * 512, (r + 1) * 512)
                dve.wait_ge(high, 3 + r)
                dve.tensor_tensor(c2s[low, at], banks[low, (2 + r) % 8, :], c2s[low, at].bitcast(F32),
                                  ALU.subtract).then_inc(done, 1)
            for t in range(4):
                low = slice(starts[2], K)
                at = slice(t * width, (t + 1) * width)
                dve.wait_ge(high, 3 + rounds + t)
                dve.tensor_tensor(zs[low, at], banks[low, 1 + t, :width], zs[low, at].bitcast(F32),
                                  ALU.subtract).then_inc(done, 1)


def hidden_layer(nc, sem, w1, x1t, c2s, zs, h_dram, ident, ident_bf, sparsity):
    inter, hidden = w1.shape
    chunks, blocks = hidden // P, inter // P
    pairs = blocks // 2
    tokens = x1t.shape[3]
    tiles = 4
    width = tokens // tiles
    tt = zs.shape[1] // P
    tail = tokens - (tt - 1) * P
    per = 2 * P // sparsity
    picks = [(a, min(4, tt - a)) for a in range(0, tt, 4)]
    NP = len(picks)
    parts = ((0, 8), (8, tt - 8))
    landed, turned = [sem(f"w1_landed{i}") for i in range(2)], sem("w1_turned")
    high, low = sem("w1_high"), sem("w1_low")
    gated, compared, masked, step = sem("gated"), sem("compared"), sem("masked"), sem("mask_step")
    mask_turned, mask_out = sem("mask_turned"), sem("mask_out")
    summed, h_out, made = sem("h_summed"), sem("h_out"), sem("keys_made")
    stored = [sem(f"h_stored{i}") for i in range(2)]
    waited = sem("gate_waited")

    with ExitStack() as mem:
        def sb(n, shape, dt=F32):
            return mem.enter_context(nc.sbuf_tensor("hid_" + n, shape, dt))

        raw = [sb(f"raw{i}", [P, hidden]) for i in range(2)]
        w = [sb(f"w{i}", [P, 2, chunks, P], F32R) for i in range(2)]
        top = sb("top", [P, tt * per])
        lead = sb("lead", [P, tt * per])
        keys = sb("keys", [P, sparsity])
        key_bf = sb("key_bf", [P, sparsity], BF16)
        equal = sb("equal", [P, tt * per, sparsity], BF16)
        mask = [sb(f"mask{i}", [P, tt * per, sparsity], BF16) for i in range(2)]
        mask_t = sb("mask_t", [P, tokens], BF16)
        h = [sb(f"h{i}", [P, tokens]) for i in range(2)]
        gate = mem.enter_context(nc.psum_tensor("gate", [P, 2, 512], F32))
        turn = mem.enter_context(nc.psum_tensor("turn", [P, 2, 512], F32))
        acc = mem.enter_context(nc.psum_tensor("hid_acc", [P, tiles, 512], F32))
        block = mem.enter_context(nc.Block())
        w1_v = w1.rearrange("(j p) n -> j p n", p=P)

        def over_pairs(eng, body):
            with eng.Fori(0, pairs // 2 - 1) as k:
                body(2 * k, 0, True)
                body(2 * k + 1, 1, True)
            body(pairs - 2, 0, True)
            body(pairs - 1, 1, False)

        @block.sync
        def _(sp):
            def load(j, p):
                sp.dma_start(raw[p][:, :], w1_v[bass.ds(j, 1)].rearrange("a p n -> (a p) n")).then_inc(landed[p], 16)

            def store(j, p):
                sp.wait_ge(h_out, tiles * (j + 2))
                sp.dma_start(h_dram[bass.ds(j, 1)].rearrange("a p n -> (a p) n"), h[p][:, :]).then_inc(stored[p], 16)

            load(0, 0)
            load(1, 1)
            with sp.Fori(0, pairs - 1) as i:
                for p in range(2):
                    sp.wait_ge(turned, 2 * (2 * i + p + 1))
                    load(2 * i + p + 2, p)
                    store(2 * i + p, p)
            store(blocks - 2, 0)
            store(blocks - 1, 1)
            for p in range(2):
                sp.wait_ge(stored[p], 16 * (pairs + 1))

        @block.gpsimd
        def _(pool):
            pool.iota(keys[:, :], [[-1, sparsity]], base=sparsity, channel_multiplier=0,
                      allow_small_or_imprecise_dtypes=True).then_inc(made, 1)
            pool.wait_ge(made, 1)
            pool.tensor_copy(key_bf[:, :], keys[:, :]).then_inc(made, 1)
            pool.sem_inc(stored[0], 16)
            pool.sem_inc(stored[1], 16)
            pool.sem_inc(h_out, tiles)
            pool.sem_inc(summed, tiles)
            pool.sem_inc(mask_out, 2)
            pool.sem_inc(compared, 1)

        @block.tensor
        def _(pe):
            def turn_w(i, p, s):
                if s == 0:
                    pe.wait_ge(landed[p], 16 * (i + 1))
                for c in range(4):
                    last = pe.transpose(turn[:, s, c * P:(c + 1) * P], raw[p][:, (4 * s + c) * P:(4 * s + c + 1) * P],
                                        ident[:, :])
                last.then_inc(turned, 1)

            def gates(i, k):
                a, n = picks[k]
                pe.wait_ge(compared, NP * i + k + 1)
                pe.sem_inc(waited, 1)
                for x in range(n):
                    last = pe.matmul(gate[:, x // 2, (x % 2) * 2 * P:(x % 2 + 1) * 2 * P],
                                     zs[:, (a + x) * P:(a + x + 1) * P], c2s[:, bass.ds(i * 2 * P, 2 * P)],
                                     start=True, stop=True)
                last.then_inc(gated, 1)

            def turn_mask(i, m, p, s):
                lo, n = parts[s]
                if p == 0 and s == 0:
                    pe.wait_ge(masked, NP * (i + 1))
                for k in range(n):
                    q = P if lo + k < tt - 1 else tail
                    at = (lo + k) * per + p * (per // 2)
                    last = pe.transpose(turn[:, s, :].bitcast(BF16)[:, k * P:k * P + q],
                                        mask[m][:q, at:at + per // 2, :].rearrange("q a b -> q (a b)"),
                                        ident_bf[:q, :q])
                last.then_inc(mask_turned, 1)

            def sums(j, p, t):
                pe.wait_ge(h_out, tiles * j + t + 1)
                product(pe, acc[:, t, :width], lambda a, c: w[p][:, a, c, :],
                        lambda a, c: x1t[:, a, c, t * width:(t + 1) * width], chunks).then_inc(summed, 1)

            def body(i, m, more):
                for p in range(2):
                    j = 2 * i + p
                    another = more or p == 0
                    pe.wait_ge(low, 2 * j + 2)
                    sums(j, p, 0)
                    if another:
                        pe.wait_ge(mask_out, 2 * j + 2)
                        turn_w(i + p, 1 - p, 0)
                    if more:
                        gates(i + 1, 2 * p)
                    sums(j, p, 1)
                    if another:
                        turn_w(i + p, 1 - p, 1)
                        pe.wait_ge(low, 2 * j + 4)
                    turn_mask(i, m, p, 0)
                    turn_mask(i, m, p, 1)
                    sums(j, p, 2)
                    if more:
                        gates(i + 1, 2 * p + 1)
                    sums(j, p, 3)

            turn_w(0, 0, 0)
            turn_w(0, 0, 1)
            for k in range(NP):
                gates(0, k)
            over_pairs(pe, body)

        @block.scalar
        def _(act):
            def high_part(j, p, s):
                act.wait_ge(turned, 2 * j + s + 1)
                act.activation(w[p][:, 0, 4 * s:4 * s + 4, :], turn[:, s, :].rearrange("q (c n) -> q c n", c=4),
                               ACT.Copy).then_inc(high, 1)

            def mask_part(j, s):
                lo, n = parts[s]
                a, e = lo * P, min((lo + n) * P, tokens)
                act.wait_ge(mask_turned, 2 * j + s + 1)
                act.wait_ge(h_out, tiles * (j + 1))
                act.activation(mask_t[:, a:e], turn[:, s, :].bitcast(BF16)[:, :e - a], ACT.Copy).then_inc(mask_out, 1)

            def body(i, m, more):
                for p in range(2):
                    j = 2 * i + p
                    if more or p == 0:
                        act.wait_ge(summed, tiles * (j + 1))
                        high_part(j + 1, 1 - p, 0)
                        high_part(j + 1, 1 - p, 1)
                    mask_part(j, 0)
                    mask_part(j, 1)

            high_part(0, 0, 0)
            high_part(0, 0, 1)
            over_pairs(act, body)

        @block.vector
        def _(dve):
            def low_part(j, p, s):
                dve.wait_ge(high, 2 * j + s + 1)
                dve.tensor_tensor(w[p][:, 1, 4 * s:4 * s + 4, :], turn[:, s, :].rearrange("q (c n) -> q c n", c=4),
                                  w[p][:, 0, 4 * s:4 * s + 4, :].bitcast(F32), ALU.subtract).then_inc(low, 1)

            def spread(ap, g):
                return ap.rearrange("q (a c) -> q a c", c=1).to_broadcast([P, g, sparsity])

            def pick(i, m, k):
                a, n = picks[k]
                g = n * per
                at = slice(a * per, a * per + g)
                done = NP * i + k
                values = gate[:, :, :].rearrange("q a (b c) -> q (a b) c", c=sparsity)[:, :g, :]
                dve.wait_ge(gated, done + 1)
                dve.tensor_reduce(top[:, at], values, AX.X, ALU.max).then_inc(step, 1)
                dve.wait_ge(step, 3 * done + 1)
                dve.tensor_tensor(equal[:, at, :], values, spread(top[:, at], g), ALU.is_equal).then_inc(compared, 1)
                dve.wait_ge(compared, done + 2)
                dve.tensor_tensor(equal[:, at, :], equal[:, at, :],
                                  key_bf[:, :].rearrange("q (a c) -> q a c", a=1).to_broadcast([P, g, sparsity]),
                                  ALU.mult).then_inc(step, 1)
                dve.wait_ge(step, 3 * done + 2)
                dve.tensor_reduce(lead[:, at], equal[:, at, :], AX.X, ALU.max).then_inc(step, 1)
                dve.wait_ge(step, 3 * done + 3)
                dve.tensor_tensor(mask[m][:, at, :], equal[:, at, :], spread(lead[:, at], g),
                                  ALU.is_equal).then_inc(masked, 1)

            def evacuate(i, p, t):
                j = 2 * i + p
                dve.wait_ge(summed, tiles * (j + 1) + t + 1)
                if t == 0:
                    dve.wait_ge(mask_out, 2 * j + 4)
                    dve.wait_ge(stored[p], 16 * (i + 1))
                at = slice(t * width, (t + 1) * width)
                dve.scalar_tensor_tensor(out=h[p][:, at], in0=acc[:, t, :width], scalar=0.0, in1=mask_t[:, at],
                                         op0=ALU.max, op1=ALU.mult).then_inc(h_out, 1)

            def body(i, m, more):
                for p in range(2):
                    j = 2 * i + p
                    if more or p == 0:
                        low_part(j + 1, 1 - p, 0)
                        low_part(j + 1, 1 - p, 1)
                    if more:
                        pick(i + 1, 1 - m, 2 * p)
                    evacuate(i, p, 0)
                    evacuate(i, p, 1)
                    if more:
                        pick(i + 1, 1 - m, 2 * p + 1)
                    evacuate(i, p, 2)
                    evacuate(i, p, 3)

            dve.wait_ge(made, 2)
            low_part(0, 0, 0)
            low_part(0, 0, 1)
            for k in range(NP):
                pick(0, 0, k)
            over_pairs(dve, body)


def project_out(nc, sem, name, left, weights, residual, out):
    chunks, _, tokens = left.shape
    cols = 512
    halves = weights.shape[1] // cols
    per = 4
    quads = chunks // per
    whole = tokens // P
    tail = tokens - whole * P
    tiles = whole + 1
    w_landed = [sem(f"{name}_w_landed{i}") for i in range(2)]
    l_landed = [sem(f"{name}_l_landed{i}") for i in range(2)]
    r_landed = [sem(f"{name}_r_landed{i}") for i in range(2)]
    stored = [sem(f"{name}_stored{i}") for i in range(2)]
    w_high, w_low = sem(name + "_w_high"), sem(name + "_w_low")
    l_high, l_low = sem(name + "_l_high"), sem(name + "_l_low")
    used, added, waited = sem(name + "_used"), sem(name + "_added"), sem(name + "_waited")
    assert whole % 2 == 0

    with ExitStack() as mem:
        def sb(n, shape, dt=F32):
            return mem.enter_context(nc.sbuf_tensor(f"{name}_{n}", shape, dt))

        w_raw = [sb(f"w_raw{i}", [P, per, cols]) for i in range(2)]
        w = sb("w", [P, 2, chunks, cols], F32R)
        l_raw = [sb(f"l_raw{i}", [P, per, P]) for i in range(2)]
        l = [sb(f"l{i}", [P, 2, per, P], F32R) for i in range(2)]
        res = [sb(f"res{i}", [P, cols]) for i in range(2)]
        y = [sb(f"y{i}", [P, cols]) for i in range(2)]
        acc = [mem.enter_context(nc.psum_tensor(f"{name}_acc{i}", [P, cols], F32)) for i in range(2)]
        block = mem.enter_context(nc.Block())
        left_v = left.rearrange("(q k) d t -> q d k t", k=per)
        w_v = weights.rearrange("(q k p) n -> q p k n", k=per, p=P)

        def over_tiles(eng, h, body):
            base = h * tiles
            body(0, base // 2, base % 2, P)
            with eng.Fori(0, (whole - 2) // 2) as i:
                for s in (1, 2):
                    body(2 * i + s, i + (base + s) // 2, (base + s) % 2, P)
            for last in (whole - 1, whole):
                body(last, (base + last) // 2, (base + last) % 2, P if last < whole else tail)

        @block.sync
        def _(sp):
            def rows_of(tt, h, rows):
                return bass.ds(tt * P, rows), slice(h * cols, (h + 1) * cols)

            def store(tt, h, i, p, rows):
                sp.wait_ge(added, 2 * i + p + 1 + 2)
                sp.sem_inc(waited, 1)
                sp.dma_start(out[rows_of(tt, h, rows)], y[p][:rows, :]).then_inc(stored[p], 16)

            for h in range(halves):
                def tile_loads(tt, i, p, rows):
                    n = 2 * i + p
                    sp.dma_start(res[p][:rows, :], residual[rows_of(tt, h, rows)]).then_inc(r_landed[p], 16)
                    for m in range(quads):
                        if isinstance(tt, int) and tt == 0:
                            sp.wait_ge(w_low, h * quads + m + 1)
                            sp.dma_start(w_raw[(h * quads + m) % 2][:, :, :],
                                         w_v[m, :, :, h * cols:(h + 1) * cols]).then_inc(w_landed[(h * quads + m) % 2], 16)
                        sp.wait_ge(l_low, n * quads + m + 1)
                        sp.sem_inc(waited, 1)
                        sp.dma_start(l_raw[(p * quads + m) % 2][:, :, :rows],
                                     left_v[m][:, :, bass.ds(tt * P, rows)]).then_inc(l_landed[(p * quads + m) % 2], 16)
                        if m == 3 and not (isinstance(i, int) and n == 0):
                            if isinstance(tt, int) and tt == 0:
                                store(whole, h - 1, i + p - 1, 1 - p, tail)
                            else:
                                store(tt - 1, h, i + p - 1, 1 - p, P)
                over_tiles(sp, h, tile_loads)
            store(whole, halves - 1, (halves * tiles - 1) // 2, (halves * tiles - 1) % 2, tail)
            for p in range(2):
                sp.wait_ge(stored[p], 16 * (1 + halves * tiles // 2))

        @block.gpsimd
        def _(pool):
            pool.sem_inc(w_low, 2)
            pool.sem_inc(l_low, 2)
            pool.sem_inc(used, 2)
            pool.sem_inc(added, 2)
            pool.sem_inc(stored[0], 16)
            pool.sem_inc(stored[1], 16)

        @block.scalar
        def _(act):
            for h in range(halves):
                def high_parts(tt, i, p, rows):
                    n = 2 * i + p
                    for m in range(quads):
                        j = p * quads + m
                        if isinstance(tt, int) and tt == 0:
                            g = h * quads + m
                            act.wait_ge(w_landed[g % 2], 16 * (g // 2 + 1))
                            if h:
                                act.wait_ge(used, 2 + ((tiles - 1) * quads + m + 1) + (h - 1) * tiles * quads)
                            act.activation(w[:, 0, m * per:(m + 1) * per], w_raw[g % 2][:, :, :],
                                           ACT.Copy).then_inc(w_high, 1)
                        act.wait_ge(l_landed[j % 2], 16 * (i * quads + j // 2 + 1))
                        act.wait_ge(used, n * quads + m + 1)
                        act.activation(l[j % 2][:, 0, :, :rows], l_raw[j % 2][:, :, :rows],
                                       ACT.Copy).then_inc(l_high, 1)
                over_tiles(act, h, high_parts)

        @block.vector
        def _(dve):
            def add(i, p, rows):
                dve.wait_ge(used, 2 + quads * (2 * i + p + 1))
                dve.wait_ge(r_landed[p], 16 * (i + 1))
                dve.wait_ge(stored[p], 16 * (i + 1))
                dve.tensor_tensor(y[p][:rows, :], acc[p][:rows, :], res[p][:rows, :], ALU.add).then_inc(added, 1)

            for h in range(halves):
                def low_parts(tt, i, p, rows):
                    n = 2 * i + p
                    for m in range(quads):
                        j = p * quads + m
                        if isinstance(tt, int) and tt == 0:
                            g = h * quads + m
                            dve.wait_ge(w_high, g + 1)
                            dve.tensor_tensor(w[:, 1, m * per:(m + 1) * per], w_raw[g % 2][:, :, :],
                                              w[:, 0, m * per:(m + 1) * per].bitcast(F32),
                                              ALU.subtract).then_inc(w_low, 1)
                        dve.wait_ge(l_high, n * quads + m + 1)
                        dve.tensor_tensor(l[j % 2][:, 1, :, :rows], l_raw[j % 2][:, :, :rows],
                                          l[j % 2][:, 0, :, :rows].bitcast(F32), ALU.subtract).then_inc(l_low, 1)
                        if m == 1 and not (isinstance(n, int) and n == 0):
                            before = tail if isinstance(tt, int) and tt == 0 else P
                            add(i + p - 1, 1 - p, before)
                over_tiles(dve, h, low_parts)
            add((halves * tiles - 1) // 2, (halves * tiles - 1) % 2, tail)

        @block.tensor
        def _(pe):
            for h in range(halves):
                def sums(tt, i, p, rows):
                    n = 2 * i + p
                    pe.wait_ge(added, n + 1)
                    for m in range(quads):
                        j = p * quads + m
                        if isinstance(tt, int) and tt == 0:
                            pe.wait_ge(w_low, h * quads + m + 1 + 2)
                        pe.wait_ge(l_low, n * quads + m + 1 + 2)
                        for k in range(per):
                            for a, c in PAIRS:
                                last = pe.matmul(acc[p][:rows, :], l[j % 2][:, a, k, :rows], w[:, c, m * per + k, :],
                                                 start=(m == 0 and k == 0 and (a, c) == PAIRS[0]),
                                                 stop=(m == quads - 1 and k == per - 1 and (a, c) == PAIRS[-1]))
                        last.then_inc(used, 1)
                over_tiles(pe, h, sums)


def cross_attention_and_sparse_ffn(nc, x, ctx, wq, wk, wv, wo, c1, c2, w1, w2t, out):
    batches, rows, hidden = x.shape
    chunks = hidden // P
    tokens = batches * rows
    d = P
    heads = wq.shape[1] // d
    groups = wk.shape[1] // d
    inter = w1.shape[0]
    rank = c1.shape[0]
    sparsity = 64
    padded = (tokens + P - 1) // P * P

    def scratch(name, shape, dt=F32):
        return nc.dram_tensor(name, shape, dt).ap()

    with ExitStack() as ctx_all:
        def sem(name):
            return ctx_all.enter_context(nc.semaphore(name))

        def sb(mem, name, shape, dt=F32):
            return mem.enter_context(nc.sbuf_tensor(name, shape, dt))

        q_dram = scratch("q_scratch", (batches, d, heads, rows))
        xt_dram = scratch("xt_scratch", (2, P, chunks, tokens))
        o_dram = scratch("o_scratch", (heads, d, tokens))
        x1_dram = scratch("x1_scratch", (batches, rows, hidden))
        h_dram = scratch("h_scratch", (inter // P, P, tokens))

        ident = sb(ctx_all, "ident", [P, P])
        ident_bf = sb(ctx_all, "ident_bf", [P, P], BF16)
        make_identity(nc, ident, ident_bf, sem("identity_made"))
        with ExitStack() as mem:
            wkv = sb(mem, "wkv", [P, 2, 2, chunks, wk.shape[1]], F32R)
            split_kv_weights(nc, sem, (wk, wv), wkv)
            with ExitStack() as mem_x:
                xt = sb(mem_x, "xt", [P, 2, chunks, tokens], F32R)
                normalise(nc, sem, "ln1", x, xt, ident)
                project_queries(nc, sem, wq, xt, q_dram, xt_dram, float(d) ** -0.5, batches, rows)
            attend(nc, sem, ctx, xt_dram, q_dram, wkv, o_dram, ident)
        project_out(nc, sem, "wo", o_dram, wo, x.rearrange("b r n -> (b r) n"),
                    x1_dram.rearrange("b r n -> (b r) n"))
        with ExitStack() as mem:
            x1t = sb(mem, "x1t", [P, 2, chunks, tokens], F32R)
            normalise(nc, sem, "ln2", x1_dram, x1t, ident)
            c2s = sb(mem, "c2s", [64 + rank, inter], F32R)
            zs = sb(mem, "zs", [64 + rank, padded], F32R)
            with ExitStack() as mem_c:
                c1t = sb(mem_c, "c1t", [P, 2, chunks, P], F32R)
                gate_weights(nc, sem, c1, c2, x1t, c1t, c2s, zs, ident)
            hidden_layer(nc, sem, w1, x1t, c2s, zs, h_dram, ident, ident_bf, sparsity)
        project_out(nc, sem, "w2", h_dram, w2t, x1_dram.rearrange("b r n -> (b r) n"),
                    out.rearrange("b r n -> (b r) n"))


_INS = ['x', 'ctx_4096', 'L0_xattn_Wq', 'L0_xattn_Wk', 'L0_xattn_Wv', 'L0_xattn_Wo',
        'L0_ffn_c1_w', 'L0_ffn_c2_w', 'L0_ffn_w1', 'L0_ffn_w2t']


def kernel(**inputs):
    import numpy as _np
    import concourse.bacc as _bacc
    from concourse import mybir as _mybir
    from concourse.bass_utils import run_bass_kernel_spmd as _run

    nc = _bacc.Bacc("TRN2", target_bir_lowering=False, num_devices=1)
    arrays, args = {}, []
    for name in _INS:
        a = _np.ascontiguousarray(inputs[name])
        arrays[f"in_{name}_dram"] = a
        args.append(nc.dram_tensor(f"in_{name}_dram", a.shape, _mybir.dt.from_np(a.dtype), kind="ExternalInput").ap())
    shape = inputs['x'].shape
    args.append(nc.dram_tensor("out_0_dram", shape, _mybir.dt.from_np(_np.dtype('float32')), kind="ExternalOutput").ap())
    cross_attention_and_sparse_ffn(nc, *args)
    r = _run(nc, [arrays], core_ids=[0])
    return r.results[0]["out_0_dram"]
```

```python
from contextlib import ExitStack

import concourse.bass as bass
from concourse import mybir

ALU = mybir.AluOpType
ACT = mybir.ActivationFunctionType
AX = mybir.AxisListType
F32 = mybir.dt.float32
F32R = mybir.dt.float32r
BF16 = mybir.dt.bfloat16

P = 128
EPS = 1e-5
PAIRS = ((0, 0), (0, 1), (1, 0))




def product(pe, out, left, right, chunks):
    for c in range(chunks):
        for a, b in PAIRS:
            last = pe.matmul(out, left(a, c), right(b, c),
                             start=(c == 0 and (a, b) == PAIRS[0]),
                             stop=(c == chunks - 1 and (a, b) == PAIRS[-1]))
    return last


def make_identity(nc, ident, ident_bf, made):
    with nc.Block() as block:
        @block.gpsimd
        def _(pool):
            pool.memset(ident[:, :], 0.0).then_inc(made, 1)
            pool.wait_ge(made, 1)
            pool.affine_select(out=ident[:, :], in_=ident[:, :], compare_op=ALU.not_equal, fill=1.0,
                               base=0, pattern=[[-1, P]], channel_multiplier=1).then_inc(made, 1)
            pool.wait_ge(made, 2)
            pool.tensor_copy(ident_bf[:, :], ident[:, :]).then_inc(made, 1)


def normalise(nc, sem, name, source, xt, ident, stats=None):
    tokens, hidden = source.shape
    chunks = hidden // P
    half = hidden // 2
    tiles = [(a, min(P, tokens - a)) for a in range(0, tokens, P)]
    NT = len(tiles)
    own = stats is None
    bounds = [0, 2] + list(range(6, NT, 4)) + [NT]
    groups = list(zip(bounds, bounds[1:]))
    R, B = 8, 4
    HEAD, SMALL = (2 if own else 1), 7
    landed = [sem(f"{name}_landed{r}") for r in range(R)]
    step, rooted, cleared = sem(name + "_step"), sem(name + "_rooted"), sem(name + "_cleared")
    ready, turned = sem(name + "_ready"), sem(name + "_turned")
    high, low = sem(name + "_high"), sem(name + "_low")

    with ExitStack() as mem:
        def sb(n, shape, dt=F32):
            return mem.enter_context(nc.sbuf_tensor(f"{name}_{n}", shape, dt))

        raw = [sb(f"raw{i}", [P, hidden]) for i in range(R)]
        if own:
            stats = sb("stats", [P, NT, 2, 6])
        moments = sb("moments", [P, NT, 2])
        small = sb("small", [P, 7, NT])
        turned_ps = [mem.enter_context(nc.psum_tensor(f"{name}_ps{i}", [P, chunks, P], F32)) for i in range(B)]
        block = mem.enter_context(nc.Block())

        @block.sync
        def _(sp):
            for t, (a, n) in enumerate(tiles):
                if t >= R:
                    sp.wait_ge(turned, t - R + 1)
                sp.dma_start(raw[t % R][:n, :], source[a:a + n, :]).then_inc(landed[t % R], 16)

        @block.gpsimd
        def _(pool):
            pool.memset(moments[:, :, :], 0.0).then_inc(cleared, 1)

        @block.vector
        def _(dve):
            def statistics(g):
                for t in range(*groups[g]):
                    n = tiles[t][1]
                    dve.wait_ge(landed[t % R], 16 * (t // R + 1))
                    for c in range(2):
                        last = dve.bn_stats(stats[:n, t, c, :], raw[t % R][:n, c * half:(c + 1) * half])
                last.then_inc(step, 1)
                dve.wait_ge(step, (HEAD + SMALL) * g + 1)

            def means(g, first, end):
                for t in range(first, end):
                    n = tiles[t][1]
                    last = dve.bn_aggr(moments[:n, t, :], stats[:n, t, :, :])
                last.then_inc(step, 1)

            def factor(g, first, end, s):
                v = [small[:, n, first:end] for n in range(7)]
                dve.wait_ge(rooted if s == 1 else step, g + 1 if s == 1 else (HEAD + SMALL) * g + HEAD + s)
                if s == 0:
                    dve.tensor_scalar(v[0], moments[:, first:end, 1], EPS, None, ALU.add).then_inc(step, 1)
                elif s == 1:
                    dve.reciprocal(v[2], v[1]).then_inc(step, 1)
                elif s == 2:
                    dve.tensor_tensor(v[3], v[2], v[2], ALU.mult).then_inc(step, 1)
                elif s == 3:
                    dve.tensor_tensor(v[4], v[3], v[0], ALU.mult).then_inc(step, 1)
                elif s == 4:
                    dve.tensor_scalar(v[3], v[4], -0.5, 1.5, ALU.mult, ALU.add).then_inc(step, 1)
                elif s == 5:
                    dve.tensor_tensor(v[5], v[2], v[3], ALU.mult).then_inc(step, 1)
                else:
                    dve.scalar_tensor_tensor(out=v[6], in0=moments[:, first:end, 0], scalar=-1.0, in1=v[5],
                                             op0=ALU.mult, op1=ALU.mult).then_inc(step, 1)

            def low_part(t):
                a, n = tiles[t]
                dve.wait_ge(high, t + 1)
                dve.tensor_tensor(xt[:, 1, :, a:a + n], turned_ps[t % B][:, :, :n],
                                  xt[:, 0, :, a:a + n].bitcast(F32), ALU.subtract).then_inc(low, 1)

            if own:
                statistics(0)
            dve.wait_ge(cleared, 1)
            first, end = groups[0] if own else (0, NT)
            means(0, first, end)
            for s in range(SMALL):
                factor(0, first, end, s)
            for g in range(len(groups)):
                more = own and g + 1 < len(groups)
                todo = list(range(SMALL))
                if more:
                    statistics(g + 1)
                    means(g + 1, *groups[g + 1])
                    factor(g + 1, *groups[g + 1], todo.pop(0))
                for t in range(*groups[g]):
                    low_part(t)
                    if more and todo:
                        factor(g + 1, *groups[g + 1], todo.pop(0))
                while more and todo:
                    factor(g + 1, *groups[g + 1], todo.pop(0))

        @block.scalar
        def _(act):
            def root(g, first, end):
                act.wait_ge(step, (HEAD + SMALL) * g + HEAD + 1)
                act.activation(small[:, 1, first:end], small[:, 0, first:end], ACT.Sqrt).then_inc(rooted, 1)

            def high_part(t):
                a, n = tiles[t]
                act.wait_ge(turned, t + 1)
                act.activation(xt[:, 0, :, a:a + n], turned_ps[t % B][:, :, :n], ACT.Copy).then_inc(high, 1)

            root(0, *(groups[0] if own else (0, NT)))
            for g, (first, end) in enumerate(groups):
                act.wait_ge(step, (HEAD + SMALL) * (g + 1 if own else 1))
                for t in range(first, end):
                    n = tiles[t][1]
                    act.wait_ge(landed[t % R], 16 * (t // R + 1))
                    act.activation(raw[t % R][:n, :], raw[t % R][:n, :], ACT.Identity,
                                   scale=small[:n, 5, t:t + 1], bias=small[:n, 6, t:t + 1]).then_inc(ready, 1)
                    if not own and t >= 2:
                        high_part(t - 2)
                if own:
                    high_part(first)
                    if g + 1 < len(groups):
                        root(g + 1, *groups[g + 1])
                    for t in range(first + 1, end):
                        high_part(t)
            if not own:
                high_part(NT - 2)
                high_part(NT - 1)

        @block.tensor
        def _(pe):
            for t, (a, n) in enumerate(tiles):
                pe.wait_ge(ready, t + 1)
                if t >= B:
                    pe.wait_ge(low, t - B + 1)
                for c in range(chunks):
                    last = pe.transpose(turned_ps[t % B][:, c, :n], raw[t % R][:n, c * P:(c + 1) * P],
                                        ident[:n, :n])
                last.then_inc(turned, 1)


def project_queries(nc, sem, wq, kv_sources, wkv, xt, q_dram, xt_dram, scale, batches, rows, stage_free, saved):
    hidden = wq.shape[0]
    chunks = hidden // P
    heads = q_dram.shape[2]
    tokens = batches * rows
    tiles, width = 4, tokens // 4
    landed = [sem(f"wq_landed{i}") for i in range(2)]
    high, low = sem("wq_high"), sem("wq_low")
    summed = sem("q_summed")
    out_act, out_dve = sem("q_out_act"), sem("q_out_dve")

    with ExitStack() as mem:
        def sb(n, shape, dt=F32):
            return mem.enter_context(nc.sbuf_tensor(n, shape, dt))

        raw = [sb(f"wq_raw{i}", [P, chunks, P]) for i in range(2)]
        w = [sb(f"wq_parts{i}", [P, 2, chunks, P], F32R) for i in range(2)]
        stage = [sb(f"q_stage{i}", [P, tokens]) for i in range(2)]
        acc = mem.enter_context(nc.psum_tensor("q_acc", [P, 2, tiles, 512], F32))
        block = mem.enter_context(nc.Block())
        wq_v = wq.rearrange("(c p) n -> p c n", p=P)
        q_v = q_dram.rearrange("b d h r -> h d b r")
        pieces = [(weight, at) for weight in range(2) for at in range(0, wkv.shape[4], P)]

        def before_head(q):
            return range(len(pieces) - 2) if q == 0 else range(len(pieces) - 2, len(pieces))

        @block.sync
        def _(sp):
            def load(h, p):
                at = slice(h * P, (h + 1) * P) if isinstance(h, int) else bass.ds(h * P, P)
                sp.dma_start(raw[p][:, :, :], wq_v[:, :, at]).then_inc(landed[p], 16)

            def store(h, p):
                sp.wait_ge(out_act, 2 * h + 2 + 4)
                sp.wait_ge(out_dve, 2 * h + 2 + 4)
                sp.dma_start(q_v[bass.ds(h, 1)].rearrange("a d b r -> (a d) b r"),
                             stage[p][:, :].rearrange("p (b r) -> p b r", b=batches)).then_inc(stage_free[p], 16)

            load(0, 0)
            load(1, 1)
            with sp.Fori(0, heads // 2 - 1) as i:
                for p in range(2):
                    sp.wait_ge(low, 2 * i + p + 1)
                    load(2 * i + p + 2, p)
                    store(2 * i + p, p)
            for n, (weight, at) in enumerate(pieces):
                sp.wait_ge(low, heads + n - 1)
                sp.dma_start(raw[n % 2][:, :, :], kv_sources[weight].rearrange(
                    "(c p) n -> p c n", p=P)[:, :, at:at + P]).then_inc(landed[n % 2], 16)
            store(heads - 2, 0)
            store(heads - 1, 1)

        @block.gpsimd
        def _(pool):
            pool.sem_inc(stage_free[0], 16)
            pool.sem_inc(stage_free[1], 16)
            pool.sem_inc(out_act, 4)
            pool.sem_inc(out_dve, 4)
            for n in range(chunks):
                part, c = n % 2, n - n % 2
                pool.wait_ge(summed, tiles * (2 * n + 1))
                pool.dma_start(xt_dram[part, :, c:c + 2], xt[:, part, c:c + 2].bitcast(F32)).then_inc(saved, 16)

        @block.scalar
        def _(act):
            def split(k, p):
                act.wait_ge(landed[p], 16 * (k + 1))
                act.activation(w[p][:, 0], raw[p][:, :, :], ACT.Copy).then_inc(high, 1)

            def evacuate(k, p):
                h = 2 * k + p
                act.wait_ge(stage_free[p], 16 * (k + 1))
                for t in (0, 2):
                    act.wait_ge(summed, tiles * h + t + 1)
                    act.activation(stage[p][:, t * width:(t + 1) * width], acc[:, p, t, :width], ACT.Copy,
                                   scale=scale).then_inc(out_act, 1)

            split(0, 0)
            split(0, 1)
            with act.Fori(0, heads // 2 - 1) as i:
                for p in range(2):
                    evacuate(i, p)
                    act.wait_ge(summed, tiles * (2 * i + p + 1))
                    split(i + 1, p)
            for q in range(2):
                for n in before_head(q):
                    weight, at = pieces[n]
                    act.wait_ge(landed[n % 2], 16 * (heads // 2 + n // 2 + 1))
                    act.activation(wkv[:, weight, 0, :, at:at + P], raw[n % 2][:, :, :], ACT.Copy).then_inc(high, 1)
                evacuate(heads // 2 - 1, q)

        @block.vector
        def _(dve):
            def split(k, p):
                dve.wait_ge(high, 2 * k + p + 1)
                dve.tensor_tensor(w[p][:, 1], raw[p][:, :, :], w[p][:, 0].bitcast(F32),
                                  ALU.subtract).then_inc(low, 1)

            def evacuate(k, p):
                h = 2 * k + p
                dve.wait_ge(stage_free[p], 16 * (k + 1))
                for t in (1, 3):
                    dve.wait_ge(summed, tiles * h + t + 1)
                    dve.tensor_scalar(stage[p][:, t * width:(t + 1) * width], acc[:, p, t, :width], scale, None,
                                      ALU.mult).then_inc(out_dve, 1)

            split(0, 0)
            split(0, 1)
            with dve.Fori(0, heads // 2 - 1) as i:
                for p in range(2):
                    evacuate(i, p)
                    split(i + 1, p)
            for q in range(2):
                for n in before_head(q):
                    weight, at = pieces[n]
                    dve.wait_ge(high, heads + n + 1)
                    dve.tensor_tensor(wkv[:, weight, 1, :, at:at + P], raw[n % 2][:, :, :],
                                      wkv[:, weight, 0, :, at:at + P].bitcast(F32), ALU.subtract).then_inc(low, 1)
                evacuate(heads // 2 - 1, q)

        @block.tensor
        def _(pe):
            with pe.Fori(0, heads // 2) as i:
                for p in range(2):
                    h = 2 * i + p
                    pe.wait_ge(low, h + 1)
                    for t in range(tiles):
                        pe.wait_ge(out_act if t % 2 == 0 else out_dve, 2 * h + t // 2 + 1)
                        product(pe, acc[:, p, t, :width], lambda a, c: w[p][:, a, c, :],
                                lambda a, c: xt[:, a, c, t * width:(t + 1) * width], chunks).then_inc(summed, 1)


def attend(nc, sem, ctx, xt_dram, q_dram, wkv, o_dram, ident, q_stored, xt_stored, o_free):
    batches, keys_ctx, hidden = ctx.shape
    _, d, heads, rows = q_dram.shape
    groups = wkv.shape[4] // d
    per = heads // groups
    chunks = hidden // P
    kv = keys_ctx + rows
    kvp = kv + kv % 2
    row_chunks = [(c * P, min(P, keys_ctx - c * P)) for c in range((keys_ctx + P - 1) // P)]
    kv_chunks = [(c * P, min(P, kv - c * P)) for c in range((kv + P - 1) // P)]
    NC = len(kv_chunks)
    full = keys_ctx // P
    cols = per * rows
    half = cols // 2
    tile = 116
    tiles = [(t * tile, min(tile, cols - t * tile)) for t in range((cols + tile - 1) // tile)]
    NT = len(tiles)
    N = groups * NT
    SB, TB, OB, KB, RB, LAG = 2, 2, 2, 2, 4, 3
    FIRST = chunks + groups
    USES = NC + chunks + groups
    half_at = [max(t for t, (a, _) in enumerate(tiles) if a < half) + 1, NT]
    STEPS = N + LAG + 4
    PARTS = 3

    def portion(count, steps, s):
        return range(count * s // steps, count * (s + 1) // steps)

    V_STEPS, T_FIRST, K_FIRST, K_STEPS = 6, 7, 9 + chunks, 4
    products = chunks * len(PAIRS)

    def v_work(i):
        return portion(NC * products, V_STEPS, i) if i < V_STEPS else ()

    def k_work(i):
        if i < K_FIRST:
            return 0, ()
        g = min((i - K_FIRST) // K_STEPS, groups - 1)
        steps = K_STEPS if g < groups - 1 else STEPS - K_FIRST - K_STEPS * (groups - 1)
        return g, portion(products, steps, i - K_FIRST - K_STEPS * g)

    def ended(i, more):
        out = [x // products for x in v_work(i) if x % products == products - 1]
        if more:
            if 0 <= i - T_FIRST < chunks:
                out.append(NC + i - T_FIRST)
            g, pieces = k_work(i)
            if products - 1 in pieces:
                out.append(NC + chunks + g)
        return out

    assert NC * P <= 512 and tile * NC <= 512 and FIRST % KB == 0 and USES % KB == 0 and N % RB == 0
    ctx_landed, lat_landed = sem("ctx_landed"), sem("lat_landed")
    q_landed = [sem(f"q_landed{i}") for i in range(2)]
    kv_full, kv_high, kv_free = sem("kv_full"), sem("kv_high"), sem("kv_free")
    q_high, q_split = sem("q_high"), sem("q_split")
    s_full, s_max, exped = sem("s_full"), sem("s_max"), sem("exped")
    inverted, scaled = sem("inverted"), sem("scaled")
    pt_full, pt_high, pt_low = sem("pt_full"), sem("pt_high"), sem("pt_low")
    o_full, o_out = sem("o_full"), sem("o_out")
    cleared, waited = sem("attend_cleared"), sem("attend_waited")

    with ExitStack() as mem:
        def sb(n, shape, dt=F32):
            return mem.enter_context(nc.sbuf_tensor(n, shape, dt))

        ctx_raw = sb("ctx_raw", [P, len(row_chunks), hidden])
        hst = sb("hst", [P, 2, chunks, kvp], F32R)
        kt = sb("kt", [P, 2, groups, kvp], F32R)
        v = sb("v", [P, 2, NC, groups * P], F32R)
        q_raw = [sb(f"q_raw{i}", [P, cols]) for i in range(2)]
        q = [sb(f"q_parts{i}", [P, 2, cols], F32R) for i in range(2)]
        probs = sb("probs", [P, RB, NC * P])
        pt = sb("pt", [P, 2, NC, cols], F32R)
        o = [sb(f"o_stage{i}", [P, cols]) for i in range(2)]
        negmax = sb("negmax", [P, RB])
        total = sb("total", [P, RB])
        inverse = sb("inverse", [P, RB])
        scores = mem.enter_context(nc.psum_tensor("scores", [P, SB, 512], F32))
        turned = mem.enter_context(nc.psum_tensor("turned", [P, TB, 512], F32))
        outs = mem.enter_context(nc.psum_tensor("outs", [P, OB, 512], F32))
        kvb = mem.enter_context(nc.psum_tensor("kvb", [P, KB, 512], F32))
        block = mem.enter_context(nc.Block())
        q_v = q_dram.rearrange("b d (g h) r -> g b d (h r)", g=groups)
        o_v = o_dram.rearrange("(g h) d (b r) -> g b d h r", g=groups, b=batches)

        def bank_of(u):
            if u >= NC + chunks:
                return kvb[:, u % KB, :kvp]
            if u >= NC:
                return kvb[:, u % KB, :keys_ctx]
            return kvb[:kv_chunks[u][1], u % KB, :]

        def part_of(u, part, dt):
            if u >= NC + chunks:
                return kt[:, part, u - NC - chunks, :].bitcast(dt)
            if u >= NC:
                return hst[:, part, u - NC, :keys_ctx].bitcast(dt)
            return v[:kv_chunks[u][1], part, u, :].bitcast(dt)

        def turned_tile(i, n):
            return turned[:, i % TB, :NC * tile].rearrange("p (k n) -> p k n", k=NC)[:, :, :n]

        @block.sync
        def _(sp):
            def load_ctx(b):
                rows_b = ctx[bass.ds(b, 1)].rearrange("a r n -> (a r) n")
                sp.dma_start(ctx_raw[:, :full, :],
                             rows_b[:full * P, :].rearrange("(c p) n -> p c n", p=P)).then_inc(ctx_landed, 16)
                sp.dma_start(ctx_raw[:keys_ctx - full * P, full, :], rows_b[full * P:, :]).then_inc(ctx_landed, 16)

            def load_latents(b):
                for part in range(2):
                    sp.dma_start(hst[:, part, :, keys_ctx:kv].bitcast(F32),
                                 xt_dram[part, :, :, bass.ds(b * rows, rows)]).then_inc(lat_landed, 16)

            def load_q(b, g):
                sp.dma_start(q_raw[g % 2][:, :],
                             q_v[g, bass.ds(b, 1)].rearrange("a d n -> (a d) n")).then_inc(q_landed[g % 2], 16)

            def store_o(b, g):
                sp.wait_ge(o_out, 2 * (groups * b + g + 1) + OB)
                sp.dma_start(o_v[g, bass.ds(b, 1)].rearrange("a d h r -> (a d) h r"),
                             o[g % 2][:, :].rearrange("p (h r) -> p h r", h=per)).then_inc(o_free[g % 2], 16)

            def batch(b, more):
                if more:
                    sp.wait_ge(kv_full, USES * b + chunks)
                    load_ctx(b + 1)
                for g in range(groups):
                    if g + 2 < groups or more:
                        sp.wait_ge(q_split, 2 * (groups * b + g + 1))
                        if g + 2 < groups:
                            load_q(b, g + 2)
                        else:
                            load_q(b + 1, g + 2 - groups)
                    if g == 1 and more:
                        sp.wait_ge(kv_full, FIRST + USES * b + NC)
                        load_latents(b + 1)
                    if g >= 2:
                        store_o(b, g - 2)
                store_o(b, groups - 2)
                store_o(b, groups - 1)

            load_ctx(0)
            sp.wait_ge(xt_stored, 16 * chunks)
            load_latents(0)
            for p in range(2):
                sp.wait_ge(q_stored[p], 16 * (heads // 2 + 1))
            load_q(0, 0)
            load_q(0, 1)
            with sp.Fori(0, batches - 1) as b:
                batch(b, True)
            batch(batches - 1, False)

        @block.gpsimd
        def _(pool):
            pool.memset(hst[:, :, :, kv:].bitcast(F32), 0.0).then_inc(cleared, 1)
            pool.memset(probs[:, :, :], 0.0).then_inc(cleared, 1)
            pool.sem_inc(kv_free, KB)
            pool.sem_inc(o_out, OB)
            pool.sem_inc(o_free[0], 16)
            pool.sem_inc(o_free[1], 16)

            def split_q(b, g, part, h):
                at = slice(h * half, (h + 1) * half)
                if part == 0 and h == 0:
                    pool.wait_ge(q_landed[g % 2], 16 * (groups // 2 * b + g // 2 + 1))
                    pool.sem_inc(waited, 1)
                if part == 0:
                    pool.tensor_scalar(q[g % 2][:, 0, at], q_raw[g % 2][:, at], 1.0, 1.0,
                                       ALU.mult, ALU.mult).then_inc(q_high, 1)
                else:
                    pool.wait_ge(q_high, 2 * (groups * b + g) + h + 1)
                    pool.tensor_tensor(q[g % 2][:, 1, at], q_raw[g % 2][:, at], q[g % 2][:, 0, at].bitcast(F32),
                                       ALU.subtract).then_inc(q_split, 1)

            def batch(b, more):
                for i in range(N):
                    g, t = divmod(i, NT)
                    n = tiles[t][1]
                    pool.wait_ge(inverted, N * b + i + 1)
                    pool.sem_inc(waited, 1)
                    pool.tensor_scalar(probs[:n, i % RB, :kv], probs[:n, i % RB, :kv], inverse[:n, i % RB:i % RB + 1],
                                       1.0, ALU.mult, ALU.mult).then_inc(scaled, 1)
                    if 1 <= t < 5:
                        piece = ((t - 1) % 2, (t - 1) // 2)
                        if g + 1 < groups:
                            split_q(b, g + 1, *piece)
                        elif more:
                            split_q(b + 1, 0, *piece)

            for h in range(2):
                for part in range(2):
                    split_q(0, 0, part, h)
            with pool.Fori(0, batches - 1) as b:
                batch(b, True)
            batch(batches - 1, False)

        @block.tensor
        def _(pe):
            def take(b, u):
                pe.wait_ge(kv_free, FIRST + USES * b + u + 1)

            def turn_ctx(c):
                u = NC + c
                for r, (a, n) in enumerate(row_chunks):
                    last = pe.transpose(kvb[:, u % KB, a:a + n], ctx_raw[:n, r, c * P:(c + 1) * P], ident[:n, :n])
                last.then_inc(kv_full, 1)

            def sum_keys(b, g, pieces):
                u = NC + chunks + g
                for x in pieces:
                    c, (a, e) = x // len(PAIRS), PAIRS[x % len(PAIRS)]
                    if x == 0:
                        take(b, u)
                    mm = pe.matmul(kvb[:, u % KB, :kvp], wkv[:, 0, a, c, g * P:(g + 1) * P], hst[:, e, c, :],
                                   start=(x == 0), stop=(x == products - 1))
                    if x == products - 1:
                        mm.then_inc(kv_full, 1)

            def sum_values(b, pieces):
                for y in pieces:
                    k, x = divmod(y, products)
                    at, n = kv_chunks[k]
                    c, (a, e) = x // len(PAIRS), PAIRS[x % len(PAIRS)]
                    if x == 0:
                        take(b, k)
                    mm = pe.matmul(kvb[:n, k % KB, :], hst[:, a, c, at:at + n], wkv[:, 1, e, c, :],
                                   start=(x == 0), stop=(x == products - 1))
                    if x == products - 1:
                        mm.then_inc(kv_full, 1)

            def score(b, i):
                g, t = divmod(i, NT)
                at, n = tiles[t]
                if t == 0:
                    pe.wait_ge(q_split, 2 * (groups * b + g + 1))
                if i >= SB:
                    pe.wait_ge(exped, N * b + i - SB + 1)
                product(pe, scores[:n, i % SB, :kvp], lambda a, c: q[g % 2][:, a, at:at + n],
                        lambda a, c: kt[:, a, g, :], 1).then_inc(s_full, 1)

            def turn(b, i):
                n = tiles[i % NT][1]
                pe.wait_ge(scaled, N * b + i + 1)
                if i >= TB:
                    pe.wait_ge(pt_low, N * b + i - TB + 1)
                for k in range(NC):
                    last = pe.transpose(turned[:, i % TB, k * tile:k * tile + n],
                                        probs[:n, i % RB, k * P:(k + 1) * P], ident[:n, :n])
                last.then_inc(pt_full, 1)

            def weigh(b, g, h, s):
                for x in portion(NC * len(PAIRS), PARTS, s):
                    k, (a, e) = x // len(PAIRS), PAIRS[x % len(PAIRS)]
                    n = kv_chunks[k][1]
                    if x == 0:
                        pe.wait_ge(pt_low, N * b + NT * g + half_at[h])
                        pe.wait_ge(o_out, 2 * (groups * b + g) + h + 1)
                    mm = pe.matmul(outs[:, h, :half], v[:n, a, k, g * P:(g + 1) * P],
                                   pt[:n, e, k, h * half:(h + 1) * half],
                                   start=(x == 0), stop=(x == NC * len(PAIRS) - 1))
                mm_last = x == NC * len(PAIRS) - 1
                if mm_last:
                    mm.then_inc(o_full, 1)

            def batch(b, more):
                for i in range(STEPS):
                    if i < N:
                        score(b, i)
                    j = i - LAG
                    for g in range(groups):
                        for h in range(2):
                            s = j - (NT * g + half_at[h] + 1)
                            if 0 <= s < PARTS:
                                if g == 0 and h == 0 and s == 0:
                                    pe.wait_ge(kv_free, FIRST + USES * b + NC + KB)
                                weigh(b, g, h, s)
                    if 0 <= j < N:
                        turn(b, j)
                    sum_values(b, v_work(i))
                    if more and 0 <= i - T_FIRST < chunks:
                        if i == T_FIRST:
                            pe.wait_ge(ctx_landed, 32 * (b + 2))
                        take(b, NC + i - T_FIRST)
                        turn_ctx(i - T_FIRST)
                    if more:
                        g, pieces = k_work(i)
                        if i == K_FIRST:
                            pe.wait_ge(kv_free, FIRST + USES * b + NC + chunks + KB)
                            pe.wait_ge(lat_landed, 32 * (b + 2))
                        sum_keys(b, g, pieces)

            pe.wait_ge(cleared, 2)
            pe.wait_ge(ctx_landed, 32)
            for c in range(chunks):
                take(-1, NC + c)
                turn_ctx(c)
            pe.wait_ge(lat_landed, 32)
            pe.wait_ge(kv_free, chunks + KB)
            for g in range(groups):
                sum_keys(-1, g, range(products))
            pe.wait_ge(kv_free, FIRST + KB)
            with pe.Fori(0, batches - 1) as b:
                batch(b, True)
            batch(batches - 1, False)

        @block.scalar
        def _(act):
            def high_part(b, u):
                act.wait_ge(kv_full, FIRST + USES * b + u + 1)
                act.activation(part_of(u, 0, F32R), bank_of(u), ACT.Copy).then_inc(kv_high, 1)

            def batch(b, more):
                for i in range(STEPS + 1):
                    j = i - LAG
                    if 0 <= j < N:
                        at, n = tiles[j % NT]
                        act.wait_ge(pt_full, N * b + j + 1)
                        act.activation(pt[:, 0, :, at:at + n], turned_tile(j, n), ACT.Copy).then_inc(pt_high, 1)
                    if i < N:
                        n = tiles[i % NT][1]
                        act.wait_ge(s_max, N * b + i + 1)
                        if i >= RB:
                            act.wait_ge(pt_full, N * b + i - RB + 1)
                        act.activation(probs[:n, i % RB, :kv], scores[:n, i % SB, :kv], ACT.Exp,
                                       bias=negmax[:n, i % RB:i % RB + 1],
                                       accum_out=total[:n, i % RB:i % RB + 1]).then_inc(exped, 1)
                    if i >= 1:
                        for u in ended(i - 1, more):
                            high_part(b, u)

            for u in range(NC, USES):
                high_part(-1, u)
            with act.Fori(0, batches - 1) as b:
                batch(b, True)
            batch(batches - 1, False)

        @block.vector
        def _(dve):
            def low_part(b, u):
                dve.wait_ge(kv_high, FIRST + USES * b + u + 1)
                dve.tensor_tensor(part_of(u, 1, F32R), bank_of(u), part_of(u, 0, F32),
                                  ALU.subtract).then_inc(kv_free, 1)

            def batch(b, more):
                for i in range(STEPS + 1):
                    if i < N:
                        n = tiles[i % NT][1]
                        dve.wait_ge(s_full, N * b + i + 1)
                        if i >= RB:
                            dve.wait_ge(exped, N * b + i - RB + 1)
                        dve.tensor_reduce(negmax[:n, i % RB:i % RB + 1], scores[:n, i % SB, :kv], AX.X, ALU.max,
                                          negate=True).then_inc(s_max, 1)
                    if 1 <= i < N + 1:
                        j = i - 1
                        n = tiles[j % NT][1]
                        dve.wait_ge(exped, N * b + j + 1)
                        if j >= RB:
                            dve.wait_ge(scaled, N * b + j - RB + 1)
                        dve.reciprocal(inverse[:n, j % RB:j % RB + 1],
                                       total[:n, j % RB:j % RB + 1]).then_inc(inverted, 1)
                    j = i - LAG
                    if 0 <= j < N:
                        at, n = tiles[j % NT]
                        dve.wait_ge(pt_high, N * b + j + 1)
                        dve.tensor_tensor(pt[:, 1, :, at:at + n], turned_tile(j, n),
                                          pt[:, 0, :, at:at + n].bitcast(F32), ALU.subtract).then_inc(pt_low, 1)
                    for g in range(groups):
                        for h in range(2):
                            if j == NT * g + half_at[h] + PARTS:
                                dve.wait_ge(o_full, 2 * (groups * b + g) + h + 1)
                                if h == 0:
                                    dve.wait_ge(o_free[g % 2], 16 * (groups // 2 * b + g // 2 + 1))
                                dve.tensor_copy(o[g % 2][:, h * half:(h + 1) * half],
                                                outs[:, h, :half]).then_inc(o_out, 1)
                    if i >= 1:
                        for u in ended(i - 1, more):
                            low_part(b, u)

            for u in range(NC, USES):
                low_part(-1, u)
            with dve.Fori(0, batches - 1) as b:
                batch(b, True)
            batch(batches - 1, False)


GATE_STARTS = (0, 32, 64)


def load_gate_weights(pool, c1, c2, c1_raw, c2_raw, cleared, landed):
    rank = c1.shape[0]
    pool.memset(c1_raw[:, :], 0.0).then_inc(cleared, 1)
    pool.memset(c2_raw[:, :, :], 0.0).then_inc(cleared, 1)
    pool.wait_ge(cleared, 2)
    for s in GATE_STARTS:
        pool.dma_start(c1_raw[s:s + rank, :], c1).then_inc(landed, 16)
        pool.dma_start(c2_raw[:, :, s:s + rank], c2.rearrange("(j p) r -> p j r", p=P)).then_inc(landed, 16)


def gate_weights(nc, sem, rank, inter, c1_raw, c2_raw, landed, x1t, c1t, c2s, zs, ident):
    hidden = c1_raw.shape[1]
    chunks, blocks = hidden // P, inter // P
    starts = GATE_STARTS
    K = starts[-1] + rank
    tokens = x1t.shape[3]
    width = tokens // 4
    per = 4
    rounds = blocks // per
    cleared = sem("gate_z_cleared")
    full, high, done = sem("gate_full"), sem("gate_high"), sem("gate_done")
    with ExitStack() as mem:
        banks = mem.enter_context(nc.psum_tensor("gate_banks", [P, 8, 512], F32))
        block = mem.enter_context(nc.Block())

        @block.gpsimd
        def _(pool):
            pool.memset(zs[:, :].bitcast(F32), 0.0).then_inc(cleared, 1)

        @block.tensor
        def _(pe):
            pe.wait_ge(landed, 32 * len(starts))
            for h in range(2):
                for c in range(4):
                    last = pe.transpose(banks[:, h, c * P:(c + 1) * P],
                                        c1_raw[:, (4 * h + c) * P:(4 * h + c + 1) * P], ident[:, :])
                last.then_inc(full, 1)
            for r in range(rounds):
                if 2 + r >= 8:
                    pe.wait_ge(done, r - 5)
                for k in range(per):
                    last = pe.transpose(banks[:, (2 + r) % 8, k * P:(k + 1) * P], c2_raw[:, per * r + k, :], ident[:, :])
                last.then_inc(full, 1)
            for t in range(4):
                pe.wait_ge(done, 2 + t)
                product(pe, banks[:, 1 + t, :width], lambda a, c: c1t[:, a, c, :],
                        lambda a, c: x1t[:, a, c, t * width:(t + 1) * width], chunks).then_inc(full, 1)

        @block.scalar
        def _(act):
            for h in range(2):
                act.wait_ge(full, h + 1)
                act.activation(c1t[:, 0, 4 * h:4 * h + 4, :], banks[:, h, :].rearrange("p (c n) -> p c n", c=4),
                               ACT.Copy).then_inc(high, 1)
            for r in range(rounds):
                act.wait_ge(full, 3 + r)
                act.activation(c2s[:, r * 512:(r + 1) * 512], banks[:K, (2 + r) % 8, :], ACT.Copy).then_inc(high, 1)
            act.wait_ge(cleared, 1)
            for t in range(4):
                act.wait_ge(full, 3 + rounds + t)
                act.activation(zs[:, t * width:(t + 1) * width], banks[:K, 1 + t, :width], ACT.Copy).then_inc(high, 1)

        @block.vector
        def _(dve):
            for h in range(2):
                dve.wait_ge(high, h + 1)
                dve.tensor_tensor(c1t[:, 1, 4 * h:4 * h + 4, :], banks[:, h, :].rearrange("p (c n) -> p c n", c=4),
                                  c1t[:, 0, 4 * h:4 * h + 4, :].bitcast(F32), ALU.subtract).then_inc(done, 1)
            for r in range(rounds):
                low = slice(starts[1], starts[1] + rank)
                at = slice(r * 512, (r + 1) * 512)
                dve.wait_ge(high, 3 + r)
                dve.tensor_tensor(c2s[low, at], banks[low, (2 + r) % 8, :], c2s[low, at].bitcast(F32),
                                  ALU.subtract).then_inc(done, 1)
            for t in range(4):
                low = slice(starts[2], K)
                at = slice(t * width, (t + 1) * width)
                dve.wait_ge(high, 3 + rounds + t)
                dve.tensor_tensor(zs[low, at], banks[low, 1 + t, :width], zs[low, at].bitcast(F32),
                                  ALU.subtract).then_inc(done, 1)


def hidden_layer(nc, sem, w1, x1t, c2s, zs, h_dram, ident, ident_bf, sparsity, stored):
    inter, hidden = w1.shape
    chunks, blocks = hidden // P, inter // P
    pairs = blocks // 2
    tokens = x1t.shape[3]
    tiles = 4
    width = tokens // tiles
    tt = zs.shape[1] // P
    tail = tokens - (tt - 1) * P
    per = 2 * P // sparsity
    picks = [(a, min(4, tt - a)) for a in range(0, tt, 4)]
    NP = len(picks)
    parts = ((0, 8), (8, tt - 8))
    landed, turned = [sem(f"w1_landed{i}") for i in range(2)], sem("w1_turned")
    high, low = sem("w1_high"), sem("w1_low")
    gated, compared, masked, step = sem("gated"), sem("compared"), sem("masked"), sem("mask_step")
    mask_turned, mask_out = sem("mask_turned"), sem("mask_out")
    summed, h_out, made = sem("h_summed"), sem("h_out"), sem("keys_made")
    waited = sem("gate_waited")

    with ExitStack() as mem:
        def sb(n, shape, dt=F32):
            return mem.enter_context(nc.sbuf_tensor("hid_" + n, shape, dt))

        raw = [sb(f"raw{i}", [P, hidden]) for i in range(2)]
        w = [sb(f"w{i}", [P, 2, chunks, P], F32R) for i in range(2)]
        top = sb("top", [P, tt * per])
        lead = sb("lead", [P, tt * per])
        keys = sb("keys", [P, sparsity])
        key_bf = sb("key_bf", [P, sparsity], BF16)
        equal = sb("equal", [P, tt * per, sparsity], BF16)
        mask = [sb(f"mask{i}", [P, tt * per, sparsity], BF16) for i in range(2)]
        mask_t = sb("mask_t", [P, tokens], BF16)
        h = [sb(f"h{i}", [P, tokens]) for i in range(2)]
        gate = mem.enter_context(nc.psum_tensor("gate", [P, 2, 512], F32))
        turn = mem.enter_context(nc.psum_tensor("turn", [P, 2, 512], F32))
        acc = mem.enter_context(nc.psum_tensor("hid_acc", [P, tiles, 512], F32))
        block = mem.enter_context(nc.Block())
        w1_v = w1.rearrange("(j p) n -> j p n", p=P)

        def over_pairs(eng, body):
            body(0, 0, True, True)
            with eng.Fori(0, pairs // 2 - 1) as k:
                body(2 * k + 1, 1, True, False)
                body(2 * k + 2, 0, True, False)
            body(pairs - 1, 1, False, False)

        @block.sync
        def _(sp):
            def load(j, p):
                sp.dma_start(raw[p][:, :], w1_v[bass.ds(j, 1)].rearrange("a p n -> (a p) n")).then_inc(landed[p], 16)

            def store(j, p):
                sp.wait_ge(h_out, tiles * (j + 2))
                sp.dma_start(h_dram[bass.ds(j, 1)].rearrange("a p n -> (a p) n"), h[p][:, :]).then_inc(stored[p], 16)

            load(0, 0)
            load(1, 1)
            with sp.Fori(0, pairs - 1) as i:
                for p in range(2):
                    sp.wait_ge(turned, 2 * (2 * i + p + 1))
                    load(2 * i + p + 2, p)
                    store(2 * i + p, p)
            store(blocks - 2, 0)
            store(blocks - 1, 1)

        @block.gpsimd
        def _(pool):
            pool.iota(keys[:, :], [[-1, sparsity]], base=sparsity, channel_multiplier=0,
                      allow_small_or_imprecise_dtypes=True).then_inc(made, 1)
            pool.wait_ge(made, 1)
            pool.tensor_copy(key_bf[:, :], keys[:, :]).then_inc(made, 1)
            pool.sem_inc(stored[0], 16)
            pool.sem_inc(stored[1], 16)
            pool.sem_inc(h_out, tiles)
            pool.sem_inc(summed, tiles)
            pool.sem_inc(mask_out, 2)
            pool.sem_inc(compared, 1)

        @block.tensor
        def _(pe):
            def turn_w(i, p, s):
                if s == 0:
                    pe.wait_ge(landed[p], 16 * (i + 1))
                for c in range(4):
                    last = pe.transpose(turn[:, s, c * P:(c + 1) * P], raw[p][:, (4 * s + c) * P:(4 * s + c + 1) * P],
                                        ident[:, :])
                last.then_inc(turned, 1)

            def gates(i, k):
                a, n = picks[k]
                pe.wait_ge(compared, NP * i + k + 1)
                pe.sem_inc(waited, 1)
                for x in range(n):
                    last = pe.matmul(gate[:, x // 2, (x % 2) * 2 * P:(x % 2 + 1) * 2 * P],
                                     zs[:, (a + x) * P:(a + x + 1) * P], c2s[:, bass.ds(i * 2 * P, 2 * P)],
                                     start=True, stop=True)
                last.then_inc(gated, 1)

            def turn_mask(i, m, p, s):
                lo, n = parts[s]
                if p == 0 and s == 0:
                    pe.wait_ge(masked, NP * (i + 1))
                for k in range(n):
                    q = P if lo + k < tt - 1 else tail
                    at = (lo + k) * per + p * (per // 2)
                    last = pe.transpose(turn[:, s, :].bitcast(BF16)[:, k * P:k * P + q],
                                        mask[m][:q, at:at + per // 2, :].rearrange("q a b -> q (a b)"),
                                        ident_bf[:q, :q])
                last.then_inc(mask_turned, 1)

            def sums(j, p, t):
                pe.wait_ge(h_out, tiles * j + t + 1)
                product(pe, acc[:, t, :width], lambda a, c: w[p][:, a, c, :],
                        lambda a, c: x1t[:, a, c, t * width:(t + 1) * width], chunks).then_inc(summed, 1)

            def body(i, m, more, first):
                for p in range(2):
                    j = 2 * i + p
                    another = more or p == 0
                    early = first and p == 0
                    late = first and p == 1
                    if early:
                        gates(0, 0)
                    pe.wait_ge(low, 2 * j + 2)
                    sums(j, p, 0)
                    if early or late:
                        gates(1 if late else 0, 1)
                    if another and not early:
                        pe.wait_ge(mask_out, 2 * j + 2)
                        turn_w(i + p, 1 - p, 0)
                    if more and not first:
                        gates(i + 1, 2 * p)
                    sums(j, p, 1)
                    if early or late:
                        gates(1 if late else 0, 2)
                    if another and not early:
                        turn_w(i + p, 1 - p, 1)
                    sums(j, p, 2)
                    if early:
                        gates(0, 3)
                        sums(j, p, 3)
                        turn_w(i + p, 1 - p, 0)
                        turn_w(i + p, 1 - p, 1)
                    if another:
                        pe.wait_ge(low, 2 * j + 4)
                    turn_mask(i, m, p, 0)
                    turn_mask(i, m, p, 1)
                    if more:
                        gates(i + 1, 0 if early else 2 * p + 1)
                    if not early:
                        sums(j, p, 3)

            turn_w(0, 0, 0)
            turn_w(0, 0, 1)
            over_pairs(pe, body)

        @block.scalar
        def _(act):
            def high_part(j, p, s):
                act.wait_ge(turned, 2 * j + s + 1)
                act.activation(w[p][:, 0, 4 * s:4 * s + 4, :], turn[:, s, :].rearrange("q (c n) -> q c n", c=4),
                               ACT.Copy).then_inc(high, 1)

            def mask_part(j, s):
                lo, n = parts[s]
                a, e = lo * P, min((lo + n) * P, tokens)
                act.wait_ge(mask_turned, 2 * j + s + 1)
                act.wait_ge(h_out, tiles * (j + 1))
                act.activation(mask_t[:, a:e], turn[:, s, :].bitcast(BF16)[:, :e - a], ACT.Copy).then_inc(mask_out, 1)

            def body(i, m, more, first):
                for p in range(2):
                    j = 2 * i + p
                    if more or p == 0:
                        act.wait_ge(summed, tiles * (j + 1))
                        high_part(j + 1, 1 - p, 0)
                        high_part(j + 1, 1 - p, 1)
                    mask_part(j, 0)
                    mask_part(j, 1)

            high_part(0, 0, 0)
            high_part(0, 0, 1)
            over_pairs(act, body)

        @block.vector
        def _(dve):
            def low_part(j, p, s):
                dve.wait_ge(high, 2 * j + s + 1)
                dve.tensor_tensor(w[p][:, 1, 4 * s:4 * s + 4, :], turn[:, s, :].rearrange("q (c n) -> q c n", c=4),
                                  w[p][:, 0, 4 * s:4 * s + 4, :].bitcast(F32), ALU.subtract).then_inc(low, 1)

            def spread(ap, g):
                return ap.rearrange("q (a c) -> q a c", c=1).to_broadcast([P, g, sparsity])

            def pick(i, m, k):
                a, n = picks[k]
                g = n * per
                at = slice(a * per, a * per + g)
                done = NP * i + k
                values = gate[:, :, :].rearrange("q a (b c) -> q (a b) c", c=sparsity)[:, :g, :]
                dve.wait_ge(gated, done + 1)
                dve.tensor_reduce(top[:, at], values, AX.X, ALU.max).then_inc(step, 1)
                dve.wait_ge(step, 3 * done + 1)
                dve.tensor_tensor(equal[:, at, :], values, spread(top[:, at], g), ALU.is_equal).then_inc(compared, 1)
                dve.wait_ge(compared, done + 2)
                dve.tensor_tensor(equal[:, at, :], equal[:, at, :],
                                  key_bf[:, :].rearrange("q (a c) -> q a c", a=1).to_broadcast([P, g, sparsity]),
                                  ALU.mult).then_inc(step, 1)
                dve.wait_ge(step, 3 * done + 2)
                dve.tensor_reduce(lead[:, at], equal[:, at, :], AX.X, ALU.max).then_inc(step, 1)
                dve.wait_ge(step, 3 * done + 3)
                dve.tensor_tensor(mask[m][:, at, :], equal[:, at, :], spread(lead[:, at], g),
                                  ALU.is_equal).then_inc(masked, 1)

            def evacuate(i, p, t):
                j = 2 * i + p
                dve.wait_ge(summed, tiles * (j + 1) + t + 1)
                if t == 0:
                    dve.wait_ge(mask_out, 2 * j + 4)
                    dve.wait_ge(stored[p], 16 * (i + 1))
                at = slice(t * width, (t + 1) * width)
                dve.scalar_tensor_tensor(out=h[p][:, at], in0=acc[:, t, :width], scalar=0.0, in1=mask_t[:, at],
                                         op0=ALU.max, op1=ALU.mult).then_inc(h_out, 1)

            def body(i, m, more, first):
                for p in range(2):
                    j = 2 * i + p
                    early = first and p == 0
                    late = first and p == 1
                    if early:
                        for k in range(NP):
                            pick(0, 0, k)
                    if late:
                        pick(1, 1 - m, 1)
                    if more or p == 0:
                        low_part(j + 1, 1 - p, 0)
                    if more and not early:
                        pick(i + 1, 1 - m, 2 * p)
                    if more or p == 0:
                        low_part(j + 1, 1 - p, 1)
                    evacuate(i, p, 0)
                    evacuate(i, p, 1)
                    if more:
                        pick(i + 1, 1 - m, 0 if early else 2 * p + 1)
                    evacuate(i, p, 2)
                    evacuate(i, p, 3)

            dve.wait_ge(made, 2)
            low_part(0, 0, 0)
            low_part(0, 0, 1)
            over_pairs(dve, body)


def project_out(nc, sem, name, left, left_stored, weights, residual, out, beside=None, stats=None):
    chunks, _, tokens = left.shape
    cols = 512
    halves = weights.shape[1] // cols
    per = 4
    quads = chunks // per
    whole = tokens // P
    tail = tokens - whole * P
    tiles = whole + 1
    w_landed = [sem(f"{name}_w_landed{i}") for i in range(2)]
    l_landed = [sem(f"{name}_l_landed{i}") for i in range(2)]
    r_landed = [sem(f"{name}_r_landed{i}") for i in range(2)]
    stored = [sem(f"{name}_stored{i}") for i in range(2)]
    w_high, w_low = sem(name + "_w_high"), sem(name + "_w_low")
    l_high, l_low = sem(name + "_l_high"), sem(name + "_l_low")
    used, added = sem(name + "_used"), sem(name + "_added")
    waited, waited_pool = sem(name + "_waited"), sem(name + "_waited_pool")
    waited_dve = sem(name + "_waited_dve")
    assert whole % 2 == 0 and halves * tiles % 2 == 0

    with ExitStack() as mem:
        def sb(n, shape, dt=F32):
            return mem.enter_context(nc.sbuf_tensor(f"{name}_{n}", shape, dt))

        w_raw = [sb(f"w_raw{i}", [P, per, cols]) for i in range(2)]
        w = sb("w", [P, 2, chunks, cols], F32R)
        l_raw = [sb(f"l_raw{i}", [P, per, P]) for i in range(2)]
        l = [sb(f"l{i}", [P, 2, per, P], F32R) for i in range(2)]
        res = [sb(f"res{i}", [P, cols]) for i in range(2)]
        y = [sb(f"y{i}", [P, cols]) for i in range(2)]
        acc = [mem.enter_context(nc.psum_tensor(f"{name}_acc{i}", [P, cols], F32)) for i in range(2)]
        block = mem.enter_context(nc.Block())
        left_v = left.rearrange("(q k) d t -> q d k t", k=per)
        w_v = weights.rearrange("(q k p) n -> q p k n", k=per, p=P)

        def over_half(eng, h, pair, body):
            base = h * tiles
            pair(base)
            with eng.Fori(0, (whole - 2) // 2) as i:
                for s in (2, 3):
                    body(2 * i + s, i + (base + s) // 2, (base + s) % 2, P)
            body(whole, (base + whole) // 2, (base + whole) % 2, tail)

        def at_tile(tt, h, rows):
            return bass.ds(tt * P, rows), slice(h * cols, (h + 1) * cols)

        @block.sync
        def _(sp):
            def load_left(tt, n, u, m, rows):
                j = n[1] * quads + u
                sp.wait_ge(l_low, 2 * quads * n[0] + j + 1)
                sp.sem_inc(waited, 1)
                sp.dma_start(l_raw[j % 2][:, :, :rows],
                             left_v[m][:, :, bass.ds(tt * P, rows)]).then_inc(l_landed[j % 2], 16)

            def load_residual(tt, h, i, p, rows):
                sp.wait_ge(added, 2 * i + p + 1)
                sp.sem_inc(waited, 1)
                sp.dma_start(res[p][:rows, :], residual[at_tile(tt, h, rows)]).then_inc(r_landed[p], 16)

            for h in range(halves):
                def pair(base):
                    for m in range(quads):
                        g = h * quads + m
                        sp.wait_ge(w_low, g + 1)
                        sp.dma_start(w_raw[g % 2][:, :, :],
                                     w_v[m, :, :, h * cols:(h + 1) * cols]).then_inc(w_landed[g % 2], 16)
                        if g == 0:
                            for before, count in left_stored:
                                sp.wait_ge(before, count)
                        load_left(0, divmod(base, 2), 2 * m, m, P)
                        load_left(1, divmod(base, 2), 2 * m + 1, m, P)
                        if m == quads // 2:
                            for t in range(2):
                                load_residual(t, h, (base + t) // 2, (base + t) % 2, P)

                def body(tt, i, p, rows):
                    for m in range(quads):
                        load_left(tt, (i, p), m, m, rows)
                        if m == quads // 2:
                            load_residual(tt, h, i, p, rows)

                over_half(sp, h, pair, body)

        @block.gpsimd
        def _(pool):
            pool.sem_inc(w_low, 2)
            pool.sem_inc(l_low, 2)
            pool.sem_inc(used, 2)
            pool.sem_inc(added, 2)
            for h in range(halves):
                def body(tt, i, p, rows):
                    pool.wait_ge(added, 2 * i + p + 1 + 2)
                    pool.sem_inc(waited_pool, 1)
                    pool.dma_start(out[at_tile(tt, h, rows)], y[p][:rows, :]).then_inc(stored[p], 16)

                def pair(base):
                    for t in range(2):
                        body(t, (base + t) // 2, (base + t) % 2, P)
                    if h == 0 and beside:
                        beside(pool)

                over_half(pool, h, pair, body)
            for p in range(2):
                pool.wait_ge(stored[p], 16 * (halves * tiles // 2))

        @block.scalar
        def _(act):
            def high_left(n, u, rows):
                j = n[1] * quads + u
                act.wait_ge(l_landed[j % 2], 16 * (n[0] * quads + j // 2 + 1))
                act.wait_ge(used, 2 * quads * n[0] + j + 1)
                act.activation(l[j % 2][:, 0, :, :rows], l_raw[j % 2][:, :, :rows], ACT.Copy).then_inc(l_high, 1)

            for h in range(halves):
                def pair(base):
                    for m in range(quads):
                        g = h * quads + m
                        act.wait_ge(w_landed[g % 2], 16 * (g // 2 + 1))
                        if h:
                            act.wait_ge(used, 2 + (base - 1) * quads + m + 1)
                        for k in range(0, per, 2):
                            act.activation(w[:, 0, m * per + k:m * per + k + 2], w_raw[g % 2][:, k:k + 2, :],
                                           ACT.Copy).then_inc(w_high, 1)
                        high_left(divmod(base, 2), 2 * m, P)
                        high_left(divmod(base, 2), 2 * m + 1, P)

                def body(tt, i, p, rows):
                    for m in range(quads):
                        high_left((i, p), m, rows)

                over_half(act, h, pair, body)

        @block.vector
        def _(dve):
            def low_left(n, u, rows):
                j = n[1] * quads + u
                dve.wait_ge(l_high, 2 * quads * n[0] + j + 1)
                dve.tensor_tensor(l[j % 2][:, 1, :, :rows], l_raw[j % 2][:, :, :rows],
                                  l[j % 2][:, 0, :, :rows].bitcast(F32), ALU.subtract).then_inc(l_low, 1)

            def add(tt, h, i, p, rows, units):
                dve.wait_ge(used, 2 + units)
                dve.wait_ge(r_landed[p], 16 * (i + 1))
                if not isinstance(i, int) or i > 0:
                    dve.wait_ge(stored[p], 16 * i)
                dve.tensor_tensor(y[p][:rows, :], acc[p][:rows, :], res[p][:rows, :], ALU.add).then_inc(added, 1)
                if stats is not None:
                    dve.wait_ge(added, 2 * i + p + 1 + 2)
                    dve.sem_inc(waited_dve, 1)
                    dve.bn_stats(stats[:rows, tt, h, :] if isinstance(tt, int)
                                 else stats[:rows, bass.ds(tt, 1), h, :].rearrange("p a n -> p (a n)"),
                                 y[p][:rows, :])

            for h in range(halves):
                def pair(base):
                    for m in range(quads):
                        g = h * quads + m
                        for k in range(0, per, 2):
                            dve.wait_ge(w_high, 2 * g + k // 2 + 1)
                            low = dve.tensor_tensor(w[:, 1, m * per + k:m * per + k + 2], w_raw[g % 2][:, k:k + 2, :],
                                                    w[:, 0, m * per + k:m * per + k + 2].bitcast(F32), ALU.subtract)
                        low.then_inc(w_low, 1)
                        low_left(divmod(base, 2), 2 * m, P)
                        if h and m == 0:
                            add(whole, h - 1, (base - 1) // 2, (base - 1) % 2, tail, base * quads)
                        low_left(divmod(base, 2), 2 * m + 1, P)
                    add(0, h, base // 2, base % 2, P, base * quads + 2 * quads - 1)

                def body(tt, i, p, rows):
                    for m in range(quads):
                        low_left((i, p), m, rows)
                        if m == 1:
                            add(tt - 1, h, i + p - 1, 1 - p, P, (2 * i + p) * quads)

                over_half(dve, h, pair, body)
            n = halves * tiles - 1
            add(whole, halves - 1, n // 2, n % 2, tail, (n + 1) * quads)

        @block.tensor
        def _(pe):
            def unit(n, u, m, p, rows):
                j = n[1] * quads + u
                pe.wait_ge(l_low, 2 * quads * n[0] + j + 1 + 2)
                for k in range(per):
                    for a, c in PAIRS:
                        last = pe.matmul(acc[p][:rows, :], l[j % 2][:, a, k, :rows], w[:, c, m * per + k, :],
                                         start=(m == 0 and k == 0 and (a, c) == PAIRS[0]),
                                         stop=(m == quads - 1 and k == per - 1 and (a, c) == PAIRS[-1]))
                last.then_inc(used, 1)

            for h in range(halves):
                def pair(base):
                    for m in range(quads):
                        pe.wait_ge(w_low, h * quads + m + 1 + 2)
                        for t in range(2):
                            if m == 0:
                                pe.wait_ge(added, base + t + 1)
                            unit(divmod(base, 2), 2 * m + t, m, (base + t) % 2, P)

                def body(tt, i, p, rows):
                    pe.wait_ge(added, 2 * i + p + 1)
                    for m in range(quads):
                        unit((i, p), m, m, p, rows)

                over_half(pe, h, pair, body)


def cross_attention_and_sparse_ffn(nc, x, ctx, wq, wk, wv, wo, c1, c2, w1, w2t, out):
    batches, rows, hidden = x.shape
    chunks = hidden // P
    tokens = batches * rows
    d = P
    heads = wq.shape[1] // d
    groups = wk.shape[1] // d
    inter = w1.shape[0]
    rank = c1.shape[0]
    sparsity = 64
    padded = (tokens + P - 1) // P * P

    def scratch(name, shape, dt=F32):
        return nc.dram_tensor(name, shape, dt).ap()

    with ExitStack() as ctx_all:
        def sem(name):
            return ctx_all.enter_context(nc.semaphore(name))

        def sb(mem, name, shape, dt=F32):
            return mem.enter_context(nc.sbuf_tensor(name, shape, dt))

        q_dram = scratch("q_scratch", (batches, d, heads, rows))
        xt_dram = scratch("xt_scratch", (2, P, chunks, tokens))
        o_dram = scratch("o_scratch", (heads, d, tokens))
        x1_dram = scratch("x1_scratch", (batches, rows, hidden))
        h_dram = scratch("h_scratch", (inter // P, P, tokens))

        ident = sb(ctx_all, "ident", [P, P])
        ident_bf = sb(ctx_all, "ident_bf", [P, P], BF16)
        make_identity(nc, ident, ident_bf, sem("identity_made"))
        with ExitStack() as mem:
            o_stored = [sem(f"o_stored{i}") for i in range(2)]
            q_stored, xt_stored = [sem(f"q_stored{i}") for i in range(2)], sem("xt_stored")
            wkv = sb(mem, "wkv", [P, 2, 2, chunks, wk.shape[1]], F32R)
            with ExitStack() as mem_x:
                xt = sb(mem_x, "xt", [P, 2, chunks, tokens], F32R)
                normalise(nc, sem, "ln1", x.rearrange("b r n -> (b r) n"), xt, ident)
                project_queries(nc, sem, wq, (wk, wv), wkv, xt, q_dram, xt_dram, float(d) ** -0.5, batches, rows,
                                q_stored, xt_stored)
            attend(nc, sem, ctx, xt_dram, q_dram, wkv, o_dram, ident, q_stored, xt_stored, o_stored)
        with ExitStack() as mem:
            gate_cleared, gate_landed = sem("gate_cleared"), sem("gate_landed")
            x1_stats = sb(mem, "x1_stats", [P, padded // P, 2, 6])
            c1_raw = sb(mem, "c1_raw", [P, hidden])
            c2_raw = sb(mem, "c2_raw", [P, inter // P, P])
            project_out(nc, sem, "wo", o_dram,
                        [(o_stored[p], 16 * (1 + groups // 2 * batches)) for p in range(2)], wo, x.rearrange("b r n -> (b r) n"),
                        x1_dram.rearrange("b r n -> (b r) n"),
                        beside=lambda pool: load_gate_weights(pool, c1, c2, c1_raw, c2_raw,
                                                              gate_cleared, gate_landed),
                        stats=x1_stats)
            x1t = sb(mem, "x1t", [P, 2, chunks, tokens], F32R)
            normalise(nc, sem, "ln2", x1_dram.rearrange("b r n -> (b r) n"), x1t, ident, x1_stats)
            c2s = sb(mem, "c2s", [GATE_STARTS[-1] + rank, inter], F32R)
            zs = sb(mem, "zs", [GATE_STARTS[-1] + rank, padded], F32R)
            with ExitStack() as mem_c:
                c1t = sb(mem_c, "c1t", [P, 2, chunks, P], F32R)
                gate_weights(nc, sem, rank, inter, c1_raw, c2_raw, gate_landed, x1t, c1t, c2s, zs, ident)
            h_stored = [sem(f"h_stored{i}") for i in range(2)]
            hidden_layer(nc, sem, w1, x1t, c2s, zs, h_dram, ident, ident_bf, sparsity, h_stored)
        project_out(nc, sem, "w2", h_dram, [(h_stored[p], 16 * (inter // P // 2 + 1)) for p in range(2)], w2t, x1_dram.rearrange("b r n -> (b r) n"),
                    out.rearrange("b r n -> (b r) n"))


_INS = ['x', 'ctx_4096', 'L0_xattn_Wq', 'L0_xattn_Wk', 'L0_xattn_Wv', 'L0_xattn_Wo',
        'L0_ffn_c1_w', 'L0_ffn_c2_w', 'L0_ffn_w1', 'L0_ffn_w2t']


def kernel(**inputs):
    import numpy as _np
    import concourse.bacc as _bacc
    from concourse import mybir as _mybir
    from concourse.bass_utils import run_bass_kernel_spmd as _run

    nc = _bacc.Bacc("TRN2", target_bir_lowering=False, num_devices=1)
    arrays, args = {}, []
    for name in _INS:
        a = _np.ascontiguousarray(inputs[name])
        arrays[f"in_{name}_dram"] = a
        args.append(nc.dram_tensor(f"in_{name}_dram", a.shape, _mybir.dt.from_np(a.dtype), kind="ExternalInput").ap())
    shape = inputs['x'].shape
    args.append(nc.dram_tensor("out_0_dram", shape, _mybir.dt.from_np(_np.dtype('float32')), kind="ExternalOutput").ap())
    cross_attention_and_sparse_ffn(nc, *args)
    r = _run(nc, [arrays], core_ids=[0])
    return r.results[0]["out_0_dram"]
```
